# Optimizing a Trainium2 kernel written in Bass

```python
import numpy as np
import jax
import jax.numpy as jnp

def _softmax(x, axis=-1):
    return jax.nn.softmax(x, axis=axis)

def _gelu(x):
    return jax.nn.gelu(x, approximate=True)

def _silu(x):
    return jax.nn.silu(x)

def _sigmoid(x):
    return jax.nn.sigmoid(x)

def _layernorm(x, axis=-1, eps=1e-05):
    m = jnp.mean(x, axis=axis, keepdims=True)
    v = jnp.var(x, axis=axis, keepdims=True)
    return (x - m) / jnp.sqrt(v + eps)

def _scatter_add(tgt, idx, src, axis=0):
    return tgt.at[idx].add(src)

def _segment_sum(src, seg, n):
    return jax.ops.segment_sum(src, seg, n)
kernel_name = 'mk_prb_d1_jaxref_r8_3d8673'

def setup_inputs(seed: int=0):
    np.random.seed(seed)
    _w = jnp.asarray

    def _L0_attn_setup():
        import jax, jax.numpy as jnp
        import numpy as np
        from jax import lax
        SPLIT = 8
        DIM = 16
        EPS = 1e-05

        def _branch(q, k, v, cw, cb, H_sp, W_sp, Hg, Wg):
            B, N, C = q.shape
            hd = C
            scale = hd ** (-0.5)
            wsz = H_sp * W_sp
            nh, nw = (Hg // H_sp, Wg // W_sp)

            def part(t):
                t = t.reshape(B, nh, H_sp, nw, W_sp, C).transpose(0, 1, 3, 2, 4, 5)
                return t.reshape(-1, wsz, 1, hd).transpose(0, 2, 1, 3)
            vimg = v.reshape(B, nh, H_sp, nw, W_sp, C).transpose(0, 1, 3, 5, 2, 4)
            vimg = vimg.reshape(-1, C, H_sp, W_sp)
            lepe = lax.conv_general_dilated(vimg, cw, (1, 1), [(1, 1), (1, 1)], dimension_numbers=('NCHW', 'OIHW', 'NCHW'), feature_group_count=C)
            lepe = lepe + cb[None, :, None, None]
            lepe = lepe.reshape(-1, 1, hd, wsz).transpose(0, 1, 3, 2)
            vw = vimg.reshape(-1, 1, hd, wsz).transpose(0, 1, 3, 2)
            attn = jax.nn.softmax(part(q) * scale @ jnp.swapaxes(part(k), -1, -2), axis=-1)
            out = attn @ vw + lepe
            out = out.transpose(0, 2, 1, 3).reshape(B, nh, nw, H_sp, W_sp, C)
            out = out.transpose(0, 1, 3, 2, 4, 5).reshape(B, N, C)
            return out
        key = jax.random.key(seed)
        ks = jax.random.split(key, 8)
        B, H, W = (8, 256, 256)
        d = DIM
        h = d // 2
        return {'x': jax.random.normal(ks[0], (B, H, W), jnp.float32), 'qkv_w': jax.random.normal(ks[1], (d, 3 * d), jnp.float32) * d ** (-0.5), 'conv_w0': jax.random.normal(ks[2], (h, 1, 3, 3), jnp.float32) * 0.3, 'conv_b0': jax.random.normal(ks[3], (h,), jnp.float32) * 0.02, 'conv_w1': jax.random.normal(ks[4], (h, 1, 3, 3), jnp.float32) * 0.3, 'conv_b1': jax.random.normal(ks[5], (h,), jnp.float32) * 0.02, 'proj_w': jax.random.normal(ks[6], (d, d), jnp.float32) * d ** (-0.5), 'proj_b': jax.random.normal(ks[7], (d,), jnp.float32) * 0.02, 'ln_w': jnp.ones((d,), jnp.float32), 'ln_b': jnp.zeros((d,), jnp.float32)}
    _L0_attn_in = _L0_attn_setup()

    def _L0_ffn_setup():
        import jax, jax.numpy as jnp
        import numpy as np
        H = 256
        I = 176
        E = 16
        G = 4
        TOPK_GROUP = 2
        TOP_K = 6
        N_SHARED = 2
        SCALE_FACTOR = 2.5
        B, S = (2, 256)

        def _gate(hs_flat, gate_weight, bias):
            T = hs_flat.shape[0]
            logits = hs_flat @ gate_weight.T
            scores = jax.nn.sigmoid(logits)
            scores_for_choice = scores + bias[None, :]
            gs = scores_for_choice.reshape(T, G, E // G)
            group_scores = jnp.sum(jax.lax.top_k(gs, 2)[0], axis=-1)
            _, group_idx = jax.lax.top_k(group_scores, TOPK_GROUP)
            group_mask = jnp.zeros((T, G), scores.dtype).at[jnp.arange(T)[:, None], group_idx].set(1.0)
            score_mask = jnp.repeat(group_mask, E // G, axis=1)
            tmp_scores = jnp.where(score_mask > 0, scores_for_choice, 0.0)
            _, topk_idx = jax.lax.top_k(tmp_scores, TOP_K)
            topk_weight = jnp.take_along_axis(scores, topk_idx, axis=1)
            topk_weight = topk_weight / (jnp.sum(topk_weight, axis=-1, keepdims=True) + 1e-20)
            topk_weight = topk_weight * SCALE_FACTOR
            return (topk_idx, topk_weight)
        key = jax.random.key(seed)
        ks = jax.random.split(key, 8)
        scale = 0.01
        SI = I * N_SHARED
        return {'hidden_states': jax.random.normal(ks[0], (B, S, H), jnp.float32), 'gate_weight': jax.random.uniform(ks[1], (E, H), jnp.float32, -0.05, 0.05), 'e_score_correction_bias': jnp.zeros((E,), jnp.float32), 'gate_proj': jax.random.normal(ks[2], (E, I, H), jnp.float32) * scale, 'up_proj': jax.random.normal(ks[3], (E, I, H), jnp.float32) * scale, 'down_proj': jax.random.normal(ks[4], (E, H, I), jnp.float32) * scale, 'shared_gate_w': jax.random.normal(ks[5], (SI, H), jnp.float32) * scale, 'shared_up_w': jax.random.normal(ks[6], (SI, H), jnp.float32) * scale, 'shared_down_w': jax.random.normal(ks[7], (H, SI), jnp.float32) * scale}
    _L0_ffn_in = _L0_ffn_setup()
    _d = {'L0_attn_x': _L0_attn_in['x'], 'L0_attn_qkv_w': _L0_attn_in['qkv_w'], 'L0_attn_conv_w0': _L0_attn_in['conv_w0'], 'L0_attn_conv_b0': _L0_attn_in['conv_b0'], 'L0_attn_conv_w1': _L0_attn_in['conv_w1'], 'L0_attn_conv_b1': _L0_attn_in['conv_b1'], 'L0_attn_proj_w': _L0_attn_in['proj_w'], 'L0_attn_proj_b': _L0_attn_in['proj_b'], 'L0_attn_ln_w': _L0_attn_in['ln_w'], 'L0_attn_ln_b': _L0_attn_in['ln_b'], 'L0_ffn_gate_weight': _L0_ffn_in['gate_weight'], 'L0_ffn_e_score_correction_bias': _L0_ffn_in['e_score_correction_bias'], 'L0_ffn_gate_proj': _L0_ffn_in['gate_proj'], 'L0_ffn_up_proj': _L0_ffn_in['up_proj'], 'L0_ffn_down_proj': _L0_ffn_in['down_proj'], 'L0_ffn_shared_gate_w': _L0_ffn_in['shared_gate_w'], 'L0_ffn_shared_up_w': _L0_ffn_in['shared_up_w'], 'L0_ffn_shared_down_w': _L0_ffn_in['shared_down_w']}
    _x0 = _d['L0_attn_x']
    _d['L0_attn_x'] = jax.random.normal(jax.random.fold_in(jax.random.key(seed), 1), (2, 1024, 256), dtype=_x0.dtype)
    del _x0
    return _d

def reference(L0_attn_x, L0_attn_qkv_w, L0_attn_conv_w0, L0_attn_conv_b0, L0_attn_conv_w1, L0_attn_conv_b1, L0_attn_proj_w, L0_attn_proj_b, L0_attn_ln_w, L0_attn_ln_b, L0_ffn_gate_weight, L0_ffn_e_score_correction_bias, L0_ffn_gate_proj, L0_ffn_up_proj, L0_ffn_down_proj, L0_ffn_shared_gate_w, L0_ffn_shared_up_w, L0_ffn_shared_down_w):

    def _L0_attn_ref(x, qkv_w, conv_w0, conv_b0, conv_w1, conv_b1, proj_w, proj_b, ln_w, ln_b):
        import jax, jax.numpy as jnp
        import numpy as np
        from jax import lax
        SPLIT = 8
        DIM = 16
        EPS = 1e-05

        def _branch(q, k, v, cw, cb, H_sp, W_sp, Hg, Wg):
            B, N, C = q.shape
            hd = C
            scale = hd ** (-0.5)
            wsz = H_sp * W_sp
            nh, nw = (Hg // H_sp, Wg // W_sp)

            def part(t):
                t = t.reshape(B, nh, H_sp, nw, W_sp, C).transpose(0, 1, 3, 2, 4, 5)
                return t.reshape(-1, wsz, 1, hd).transpose(0, 2, 1, 3)
            vimg = v.reshape(B, nh, H_sp, nw, W_sp, C).transpose(0, 1, 3, 5, 2, 4)
            vimg = vimg.reshape(-1, C, H_sp, W_sp)
            lepe = lax.conv_general_dilated(vimg, cw, (1, 1), [(1, 1), (1, 1)], dimension_numbers=('NCHW', 'OIHW', 'NCHW'), feature_group_count=C)
            lepe = lepe + cb[None, :, None, None]
            lepe = lepe.reshape(-1, 1, hd, wsz).transpose(0, 1, 3, 2)
            vw = vimg.reshape(-1, 1, hd, wsz).transpose(0, 1, 3, 2)
            attn = jax.nn.softmax(part(q) * scale @ jnp.swapaxes(part(k), -1, -2), axis=-1)
            out = attn @ vw + lepe
            out = out.transpose(0, 2, 1, 3).reshape(B, nh, nw, H_sp, W_sp, C)
            out = out.transpose(0, 1, 3, 2, 4, 5).reshape(B, N, C)
            return out
        B, H, W = x.shape
        Hg, Wg = (H // 4, W // 4)
        C = DIM
        tok = x.reshape(B, H * W // C, C)
        qkv = (tok @ qkv_w).reshape(B, -1, 3, C)
        q, k, v = (qkv[:, :, 0], qkv[:, :, 1], qkv[:, :, 2])
        h = C // 2
        x1 = _branch(q[..., :h], k[..., :h], v[..., :h], conv_w0, conv_b0, 1, SPLIT, Hg, Wg)
        x2 = _branch(q[..., h:], k[..., h:], v[..., h:], conv_w1, conv_b1, SPLIT, 1, Hg, Wg)
        att = jnp.concatenate([x1, x2], axis=-1) @ proj_w + proj_b
        mu = att.mean(-1, keepdims=True)
        var = ((att - mu) ** 2).mean(-1, keepdims=True)
        normed = (att - mu) * lax.rsqrt(var + EPS) * ln_w + ln_b
        tok = tok + normed
        return jnp.transpose(tok, (0, 2, 1)).reshape(B, H, W)

    def _L0_ffn_ref(hidden_states, gate_weight, e_score_correction_bias, gate_proj, up_proj, down_proj, shared_gate_w, shared_up_w, shared_down_w):
        import jax, jax.numpy as jnp
        import numpy as np
        H = 256
        I = 176
        E = 16
        G = 4
        TOPK_GROUP = 2
        TOP_K = 6
        N_SHARED = 2
        SCALE_FACTOR = 2.5
        B, S = (2, 256)

        def _gate(hs_flat, gate_weight, bias):
            T = hs_flat.shape[0]
            logits = hs_flat @ gate_weight.T
            scores = jax.nn.sigmoid(logits)
            scores_for_choice = scores + bias[None, :]
            gs = scores_for_choice.reshape(T, G, E // G)
            group_scores = jnp.sum(jax.lax.top_k(gs, 2)[0], axis=-1)
            _, group_idx = jax.lax.top_k(group_scores, TOPK_GROUP)
            group_mask = jnp.zeros((T, G), scores.dtype).at[jnp.arange(T)[:, None], group_idx].set(1.0)
            score_mask = jnp.repeat(group_mask, E // G, axis=1)
            tmp_scores = jnp.where(score_mask > 0, scores_for_choice, 0.0)
            _, topk_idx = jax.lax.top_k(tmp_scores, TOP_K)
            topk_weight = jnp.take_along_axis(scores, topk_idx, axis=1)
            topk_weight = topk_weight / (jnp.sum(topk_weight, axis=-1, keepdims=True) + 1e-20)
            topk_weight = topk_weight * SCALE_FACTOR
            return (topk_idx, topk_weight)
        b, s, h = hidden_states.shape
        hs = hidden_states.reshape(-1, h)
        T = hs.shape[0]
        topk_idx, topk_weight = _gate(hs, gate_weight, e_score_correction_bias)
        comb = jnp.zeros((T, E), hs.dtype).at[jnp.arange(T)[:, None], topk_idx].add(topk_weight)
        out = jnp.zeros_like(hs)
        for e in range(E):
            g = hs @ gate_proj[e].T
            u = hs @ up_proj[e].T
            inter = jax.nn.silu(g) * u
            out = out + comb[:, e:e + 1] * (inter @ down_proj[e].T)
        y = out.reshape(b, s, h)
        sg = hidden_states @ shared_gate_w.T
        su = hidden_states @ shared_up_w.T
        shared_out = jax.nn.silu(sg) * su @ shared_down_w.T
        return y + shared_out
    x = L0_attn_x
    xn = _layernorm(x, axis=-1)
    x = x + _L0_attn_ref(xn, L0_attn_qkv_w, L0_attn_conv_w0, L0_attn_conv_b0, L0_attn_conv_w1, L0_attn_conv_b1, L0_attn_proj_w, L0_attn_proj_b, L0_attn_ln_w, L0_attn_ln_b) + _L0_ffn_ref(xn, L0_ffn_gate_weight, L0_ffn_e_score_correction_bias, L0_ffn_gate_proj, L0_ffn_up_proj, L0_ffn_down_proj, L0_ffn_shared_gate_w, L0_ffn_shared_up_w, L0_ffn_shared_down_w)
    return x

_drawn_inputs = setup_inputs


def setup_inputs(seed=0):
    import zlib

    import numpy as np

    out = dict(_drawn_inputs(seed))
    spreads = {'L0_attn_ln_w': (1.0, 0.2),
     'L0_attn_ln_b': (0.0, 0.1),
     'L0_ffn_e_score_correction_bias': (0.0, 0.8)}
    factors = {'L0_attn_conv_b1': 3.861,
     'L0_attn_proj_b': 2.912,
     'L0_ffn_gate_weight': 8.0,
     'L0_ffn_gate_proj': 8.0,
     'L0_ffn_up_proj': 8.0,
     'L0_ffn_down_proj': 8.0,
     'L0_ffn_shared_gate_w': 8.0,
     'L0_ffn_shared_up_w': 8.0,
     'L0_ffn_shared_down_w': 8.0,
     'L0_attn_conv_b0': 3.847}
    for name, (base, spread) in spreads.items():
        noise = np.random.default_rng([zlib.crc32(name.encode()), seed]).standard_normal(out[name].shape)
        drawn = base * np.exp(spread * noise) if base else spread * noise
        out[name] = jnp.asarray(drawn.astype(out[name].dtype))
    for name, factor in factors.items():
        out[name] = (out[name] * factor).astype(out[name].dtype)
    return out
```

```python
from contextlib import ExitStack

import concourse.bass as bass
from concourse import mybir

F32 = mybir.dt.float32
F32R = mybir.dt.float32r
ALU = mybir.AluOpType
ACT = mybir.ActivationFunctionType
AX = mybir.AxisListType

P = 128
B = 2
ROWS = 1024
H = 256
KT = H // P
T = B * ROWS
C = 16
TOK = H // C
WIN = 8
HD = C // 2
NE = 16
TOP = 6
I = 176
SI = 2 * I
NBLK = 4
BT = T // NBLK
TILES = BT // P
SHARED = -(-SI // P)
ROUTED = NE * I // P
MT = SHARED + ROUTED
UP = 2 * KT * P
WTILE = UP + H
SLOTS = 8
RAW = 3
LN_EPS = 1e-5
GROUPS = [(0, 3), (3, 6), (9, 6), (15, 6), (21, 4)]
COMBO = 3 * HD * P
C_QKV, C_PROJ, C_GATE = 0, 3 * C, 4 * C
C_ROW = C_GATE + KT * NE
R_BIAS, R_LNW, R_LNB, R_PB, R_CW, R_CB = 0, NE, NE + C, NE + 2 * C, NE + 3 * C, NE + 3 * C + 6 * HD
CONSTS = C_ROW + R_CB + 2 * HD


def first_unit(g):
    return sum(n for _, n in GROUPS[:g]) * NBLK


def last_unit(tile):
    g = max(g for g in range(len(GROUPS)) if GROUPS[g][0] <= tile)
    m0, n = GROUPS[g]
    return first_unit(g) + n * (NBLK - 1) + tile - m0


def early_splits(u):
    tile = GROUPS[1][0] + u
    if tile < SLOTS:
        return [tile]
    return [t for t in range(SLOTS, GROUPS[1][0] + GROUPS[1][1]) if last_unit(t - SLOTS) + 1 == u]


class Tally:

    def __init__(self):
        self.n, self.it, self.per = 0, None, 0

    def add(self, k=1):
        self.n += k
        return self.value()

    def value(self):
        return self.n if self.it is None else self.n + self.it * self.per

    def enter(self, it, per):
        self.it, self.per, self.start = it, per, self.n

    def leave(self, times):
        assert self.n - self.start == self.per, (self.n - self.start, self.per)
        self.n += self.per * (times - 1)
        self.it = None


def segments(tile):
    row = (tile - SHARED) * P
    e = row // I
    cut = min(P, (e + 1) * I - row)
    if cut == P:
        return [(0, P // 2, e), (P // 2, P, e)]
    return [(0, cut, e), (cut, P, e + 1)]


def build(nc, x, wall, consts, out):
    ctx = ExitStack()
    with ctx:
        def sb(name, shape, dt=F32):
            return ctx.enter_context(nc.sbuf_tensor(name, shape, dt))

        def sem(name):
            return ctx.enter_context(nc.semaphore(name))

        comb_dram = nc.dram_tensor("comb_dram", [NE, T], F32).ap()
        xn_dram = nc.dram_tensor("xn_dram", [P, TOK * H], F32).ap()

        xpix = sb("xpix", [P, TOK * H])
        yacc = sb("yacc", [P, TOK * H])
        xT_hi = sb("xT_hi", [P, KT, T], F32R)
        xT_lo = sb("xT_lo", [P, KT, T], F32R)
        qkv = sb("qkv", [P, 2 * B * COMBO])
        w_hi = sb("w_hi", [P, SLOTS, WTILE], F32R)
        w_lo = sb("w_lo", [P, SLOTS, WTILE], F32R)
        raw = sb("raw", [P, RAW, WTILE])
        comb = sb("comb", [P, 2, BT])
        sil = sb("sil", [P, 2, BT])
        inter = sb("inter", [P, 2, BT])
        in_hi = sb("in_hi", [P, 2, BT], F32R)
        in_lo = sb("in_lo", [P, 2, BT], F32R)
        prod = sb("prod", [P, 2, HD * P])
        cst = sb("cst", [P, CONSTS])
        ident = sb("ident", [P, P])
        mask8 = sb("mask8", [P, WIN])
        blk_hi = sb("blk_hi", [P, 3 * C * WIN], F32R)
        blk_lo = sb("blk_lo", [P, 3 * C * WIN], F32R)
        pblk = sb("pblk", [P, P])
        prow = sb("prow", [1, P])
        ones = sb("ones", [1, P])
        gw2 = sb("gw2", [P, KT, 2 * NE], F32R)
        combT = sb("combT", [P, 2, P])
        stats = sb("stats", [P, TOK, 6])
        mv = sb("mv", [P, TOK, 2])
        rstd = sb("rstd", [P, TOK])
        expo = sb("expo", [P, P])
        mx = sb("mx", [P, 2, P])

        guA = [ctx.enter_context(nc.psum_tensor(f"gate{i}", [P, BT], F32)) for i in range(2)]
        guB = [ctx.enter_context(nc.psum_tensor(f"up{i}", [P, BT], F32)) for i in range(2)]
        ps_y = ctx.enter_context(nc.psum_tensor("ps_y", [P, TILES * H], F32))
        misc = [ctx.enter_context(nc.psum_tensor(f"misc{i}", [P, 512], F32)) for i in range(2)]

        x_in = [sem(f"x_in{i}") for i in range(4)]
        cst_in, yacc_in, xn_out, comb_out = sem("cst_in"), sem("yacc_in"), sem("xn_out"), sem("comb_out")
        xn_in, out_done = sem("xn_in"), sem("out_done")
        raw_in = [sem(f"raw_in{i}") for i in range(RAW)]
        comb_in = [sem(f"comb_in{i}") for i in range(2)]
        masks, gen, stat, rstd_ok, xn_ok = sem("masks"), sem("gen"), sem("stat"), sem("rstd_ok"), sem("xn_ok")
        blk_ok, tp, hi_ok, lo_ok = sem("blk_ok"), sem("tp"), sem("hi_ok"), sem("lo_ok")
        logit_ok, sig_in, sig_ok, route_ok, combT_ok, combT_sb = (
            sem("logit_ok"), sem("sig_in"), sem("sig_ok"), sem("route_ok"), sem("combT_ok"), sem("combT_sb"))
        qkv_ps, qkv_ok = sem("qkv_ps"), sem("qkv_ok")
        wsplit_hi, wsplit_lo = sem("wsplit_hi"), sem("wsplit_lo")
        g_ps, u_ps, sil_ok, t_ok, m_ok, ihi_ok, ilo_ok = (
            sem("g_ps"), sem("u_ps"), sem("sil_ok"), sem("t_ok"), sem("m_ok"), sem("ihi_ok"), sem("ilo_ok"))
        d_ok, y_ps, y_ok = sem("d_ok"), sem("y_ps"), sem("y_ok")
        step, sub_ok, exp_ok, att_ok, attx_ok = sem("step"), sem("sub_ok"), sem("exp_ok"), sem("att_ok"), sem("attx_ok")
        at_ps, at_sb, z_ps, z_sb = sem("at_ps"), sem("at_sb"), sem("z_ps"), sem("z_sb")
        lnv_ok, lnr_ok, sq_ok, zc_ok = sem("lnv_ok"), sem("lnr_ok"), sem("sq_ok"), sem("zc_ok")

        row = cst[:, C_ROW:CONSTS]
        xw = xpix[:, :].rearrange("p (m w) -> p m w", m=TOK)
        attT = qkv[:, 0:4096].rearrange("p (h m b r) -> p h m b r", h=2, m=16, b=B)
        Z = qkv[:, 4096:8192]
        xn2 = qkv[:, 8192:12288]
        x_pix = x.rearrange("b (k m) w -> (b k) (m w)", m=TOK)

        xW_hi, xW_lo = (w[:, 2:SLOTS, :].rearrange("p s w -> p (s w)")[:, 0:KT * T].rearrange("p (k t) -> p k t", k=KT)
                        for w in (w_hi, w_lo))

        def by_stream(ap, k, j):
            return ap[:, k, :].rearrange("p (c b q m) -> p m b c q", c=16, b=B, q=4)[:, j]

        def by_window(ap, k, j):
            return ap[:, k, :].rearrange("p (b e i w a) -> p i a b w e", b=B, e=2, i=4, a=4)[:, j // 4, j % 4]

        block = ctx.enter_context(nc.Block())

        @block.sync
        def _(sp):
            def load_raw(m):
                if m >= RAW:
                    sp.wait_ge(wsplit_hi, m - RAW + 1)
                    sp.wait_ge(wsplit_lo, m - RAW + 1)
                sp.dma_start(raw[:, m % RAW, :], wall[m]).then_inc(raw_in[m % RAW], 16)

            for q in range(4):
                sp.dma_start(xpix[:, q * 1024:(q + 1) * 1024], x_pix[:, q * 1024:(q + 1) * 1024]).then_inc(x_in[q], 16)
                if q == 0:
                    sp.dma_start(cst[:, :], consts).then_inc(cst_in, 16)
            for m in range(RAW):
                load_raw(m)
            sp.wait_ge(xn_ok, TOK)
            sp.dma_start(xn_dram, xpix[:, :]).then_inc(xn_out, 16)
            sp.wait_ge(route_ok, 1)
            for b in range(B):
                sp.dma_start(yacc[64 * b:64 * b + 64, :].rearrange("p (c w) -> p c w", c=C),
                             x[b].rearrange("(c r) w -> r c w", c=C)).then_inc(yacc_in, 16)
            for m in range(RAW, GROUPS[1][0] + GROUPS[1][1]):
                load_raw(m)
            sp.wait_ge(combT_sb, 1)
            sp.dma_start(comb_dram.rearrange("(h e) (c p) -> (e c) h p", h=2, p=P), combT[:, :, :]).then_inc(comb_out, 16)
            sp.wait_ge(comb_out, 16)
            for g in range(1, 5):
                m0, n = GROUPS[g]
                r0 = first_unit(g) - first_unit(1)
                def comb_block(b, last, slots_new):
                    for i in range(n):
                        if not (slots_new and i < 2):
                            sp.wait_ge(t_ok, r0 + n * b + i - 1)
                        for p0, p1, e in segments(m0 + i):
                            sp.dma_start(comb[p0:p1, i % 2, :],
                                         comb_dram[e:e + 1, bass.ds(b * BT, BT)].to_broadcast([p1 - p0, BT])
                                         ).then_inc(comb_in[i % 2], 16)
                        if last and g < 4 and i < GROUPS[g + 1][1]:
                            load_raw(m0 + n + i)
                comb_block(0, False, g == 1)
                with sp.Fori(1, NBLK - 1) as b:
                    comb_block(b, False, False)
                comb_block(NBLK - 1, True, False)
            sp.wait_ge(xn_out, 16)
            sp.wait_ge(attx_ok, 4)
            sp.dma_start(xn2, xn_dram).then_inc(xn_in, 16)
            for b in range(NBLK):
                sp.wait_ge(y_ok, 5 * NBLK)
                for s in range(B):
                    sp.dma_start(out[s].rearrange("(c r) w -> r c w", c=C)[:, TILES * b:TILES * (b + 1), :],
                                 yacc[64 * s:64 * s + 64, b * 1024:(b + 1) * 1024].rearrange("p (c w) -> p c w", c=TILES)
                                 ).then_inc(out_done, 16)
            sp.wait_ge(out_done, 16 * B * NBLK)

        @block.gpsimd
        def _(pool):
            nc.gpsimd.memset(ident[:, :], 0.0).then_inc(gen, 1)
            nc.gpsimd.memset(mask8[:, :], 1.0).then_inc(gen, 1)
            nc.gpsimd.memset(ones[:, :], 1.0).then_inc(masks, 1)
            nc.gpsimd.memset(expo[:, :], -0.5).then_inc(gen, 1)
            pool.wait_ge(gen, 3)
            nc.gpsimd.affine_select(out=ident[:, :], in_=ident[:, :], compare_op=ALU.not_equal, fill=1.0, base=0,
                                    pattern=[[-1, P]], channel_multiplier=1).then_inc(masks, 1)
            nc.gpsimd.affine_select(out=mask8[:, :], in_=mask8[:, :], compare_op=ALU.is_ge, fill=0.0, base=0,
                                    pattern=[[-C, WIN]], channel_multiplier=1).then_inc(gen, 1)
            pool.wait_ge(gen, 4)
            nc.gpsimd.affine_select(out=mask8[:, :], in_=mask8[:, :], compare_op=ALU.is_ge, fill=0.0, base=C - 1,
                                    pattern=[[C, WIN]], channel_multiplier=-1).then_inc(masks, 1)
            for q in range(4):
                pool.wait_ge(stat, q + 1)
                nc.gpsimd.tensor_tensor(rstd[:, 4 * q:4 * q + 4], mv[:, 4 * q:4 * q + 4, 1], expo[:, 0:4], ALU.pow
                                        ).then_inc(rstd_ok, 1)

            def split_lo(m):
                s = m % SLOTS
                pool.wait_ge(wsplit_hi, m + 1)
                nc.gpsimd.tensor_tensor(w_lo[:, s, :], raw[:, m % RAW, :], w_hi[:, s, :].bitcast(F32), ALU.subtract
                                        ).then_inc(wsplit_lo, 1)

            def lo(u, par):
                pool.wait_ge(ihi_ok, u + 1)
                nc.gpsimd.tensor_tensor(in_lo[:, par, :], inter[:, par, :], in_hi[:, par, :].bitcast(F32), ALU.subtract
                                        ).then_inc(ilo_ok, 1)

            for m in range(RAW):
                split_lo(m)
            for u in range(first_unit(1)):
                if u:
                    lo(u - 1, (u - 1) % 2)
                for m in early_splits(u):
                    split_lo(m)
            for g in range(1, 5):
                m0, n = GROUPS[g]
                U0 = first_unit(g)

                def unit_block(b, last):
                    for i in range(n):
                        u = U0 + n * b + i
                        r = u - first_unit(1)
                        pool.wait_ge(sil_ok, u + 1)
                        pool.wait_ge(comb_in[i % 2], (U0 - first_unit(1)) * 16 + n * 16 * b + 32 * (i // 2 + 1))
                        nc.gpsimd.tensor_tensor(sil[:, i % 2, :], sil[:, i % 2, :], comb[:, i % 2, :], ALU.mult
                                                ).then_inc(t_ok, 1)
                        lo(u - 1, (i + 1) % 2)
                        if last and g < 4 and i < GROUPS[g + 1][1]:
                            split_lo(m0 + n + i)
                with pool.Fori(0, NBLK - 1) as b:
                    unit_block(b, False)
                unit_block(NBLK - 1, True)
            lo(first_unit(5) - 1, 1)
            for hf in range(2):
                pool.wait_ge(lnv_ok, hf + 1)
                nc.gpsimd.tensor_tensor(mx[:, hf, :], mx[:, hf, :], expo[:, 0:P], ALU.pow).then_inc(lnr_ok, 1)

        @block.scalar
        def _(act):
            def split_hi(m):
                act.wait_ge(raw_in[m % RAW], 16 * (m // RAW + 1))
                if m >= SLOTS:
                    act.wait_ge(d_ok, last_unit(m - SLOTS) + 1)
                nc.scalar.activation(w_hi[:, m % SLOTS, :], raw[:, m % RAW, :], ACT.Copy).then_inc(wsplit_hi, 1)

            for j in range(TOK):
                act.wait_ge(tp, j + 1)
                for k in range(KT):
                    src = misc[j % 2][:, k * P:(k + 1) * P]
                    nc.scalar.activation(by_stream(xT_hi, k, j), src.rearrange("p (b c q) -> p b c q", b=B, q=4), ACT.Copy)
                    last = nc.scalar.activation(by_window(xW_hi, k, j), src.rearrange("p (b w e) -> p b w e", b=B, e=2),
                                                ACT.Copy)
                last.then_inc(hi_ok, 1)
            for m in range(2):
                split_hi(m)
            act.wait_ge(sig_in, 1)
            nc.scalar.activation(prod[:, 0, 256:512], prod[:, 0, 0:256], ACT.Sigmoid).then_inc(sig_ok, 1)
            for bt in range(B):
                for i in range(WIN):
                    for jh in range(2):
                        n = (bt * WIN + i) * 2 + jh
                        act.wait_ge(qkv_ps, n + 1)
                        src = misc[n % 2][:, 0:3 * C * WIN].rearrange("p (t r d j) -> p r t d j", t=3, r=2, j=WIN)
                        for br in range(2):
                            c0 = (bt * 2 + br) * COMBO
                            dst = qkv[:, c0:c0 + COMBO].rearrange("p (t d k) -> p t d k", t=3, d=HD)
                            if br == 0:
                                dst = dst[:, :, :, i * 16 + jh * 8:i * 16 + jh * 8 + 8]
                            else:
                                dst = dst.rearrange("p t d (j i) -> p i t d j", i=WIN)[:, i, :, :, jh * 8:jh * 8 + 8]
                            last = nc.scalar.activation(dst, src[:, br], ACT.Copy)
                        last.then_inc(qkv_ok, 1)
            split_hi(2)

            def silu(u, par, early):
                act.wait_ge(g_ps, u + 1)
                if not early:
                    act.wait_ge(m_ok, u - 1)
                nc.scalar.activation(sil[:, par, :], guA[par][:, :], ACT.Silu).then_inc(sil_ok, 1)

            def hi(u, par, early):
                act.wait_ge(m_ok, u + 1)
                if not early:
                    act.wait_ge(d_ok, u - 1)
                nc.scalar.activation(in_hi[:, par, :], inter[:, par, :], ACT.Copy).then_inc(ihi_ok, 1)

            for u in range(first_unit(1)):
                silu(u, u % 2, u < 2)
                if u:
                    hi(u - 1, (u - 1) % 2, u < 3)
                if u == COMB_AT + 1:
                    act.wait_ge(combT_ok, 1)
                    nc.scalar.activation(combT[:, :, :], misc[0][:, 0:2 * P].rearrange("p (h q) -> p h q", h=2),
                                         ACT.Copy).then_inc(combT_sb, 1)
                for m in early_splits(u):
                    split_hi(m)
            for g in range(1, 5):
                m0, n = GROUPS[g]
                U0 = first_unit(g)

                def unit_block(b, last, extra):
                    for i in range(n):
                        u = U0 + n * b + i
                        silu(u, i % 2, False)
                        hi(u - 1, (i + 1) % 2, False)
                        if last and g < 4 and i < GROUPS[g + 1][1]:
                            split_hi(m0 + n + i)
                        if g == 2 and i == 1:
                            act.wait_ge(sub_ok, b + 1)
                            sc = xpix[:, bass.ds(b * 1024, 1024)]
                            nc.scalar.activation(sc, sc, ACT.Exp, scale=HD ** -0.5).then_inc(exp_ok, 1)
                        if extra:
                            extra(n * b + i)
                if g < 4:
                    with act.Fori(0, NBLK - 1) as b:
                        unit_block(b, False, None)
                    unit_block(NBLK - 1, True, None)
                else:
                    def tail_step(s):
                        if s == 0:
                            act.wait_ge(att_ok, 4)
                            for cb in range(4):
                                bt, br = divmod(cb, 2)
                                src = qkv[:, cb * COMBO:cb * COMBO + HD * P]
                                dst = xpix[:, bt * 2048:(bt + 1) * 2048].rearrange(
                                    "p (i j r d) -> p r d i j", i=WIN, j=16, r=2)[:, br]
                                if br == 0:
                                    src = src.rearrange("p (d i j) -> p d i j", d=HD, i=WIN)
                                else:
                                    src = src.rearrange("p (d j i) -> p d i j", d=HD, i=WIN)
                                nc.scalar.activation(dst, src, ACT.Copy).then_inc(attx_ok, 1)
                        for j in transposes_at(s - 1):
                            bt, i = divmod(j, WIN)
                            act.wait_ge(at_ps, j + 1)
                            src = misc[j % 2][:, 0:2 * P].rearrange("p (h r a) -> p h a r", h=2, a=4)
                            dst = attT[:, :, 4 * (i % 4):4 * (i % 4) + 4, bt, :].rearrange(
                                "p h a (r e) -> p e h a r", e=2)[:, i // 4]
                            nc.scalar.activation(dst, src, ACT.Copy).then_inc(at_sb, 1)
                        for j in projections_at(s - 1):
                            act.wait_ge(z_ps, j + 1)
                            nc.scalar.activation(Z[:, j * 512:(j + 1) * 512], misc[j % 2][:, :], ACT.Copy).then_inc(z_sb, 1)
                    for b in range(NBLK):
                        unit_block(b, b == NBLK - 1, tail_step)
            hi(first_unit(5) - 1, 1, False)
            for hf in range(2):
                act.wait_ge(zc_ok, hf + 1)
                nc.scalar.activation(xpix[:, hf * 2048:(hf + 1) * 2048], Z[:, hf * 2048:(hf + 1) * 2048], ACT.Square
                                     ).then_inc(sq_ok, 1)

        @block.tensor
        def _(pe):
            pe.wait_ge(masks, 3)
            for j in range(TOK):
                pe.wait_ge(xn_ok, j + 1)
                if j >= 2:
                    pe.wait_ge(hi_ok, j - 1)
                    pe.wait_ge(lo_ok, j - 1)
                for k in range(KT):
                    last = nc.tensor.transpose(misc[j % 2][:, k * P:(k + 1) * P], xw[:, j, k * P:(k + 1) * P], ident[:, :])
                last.then_inc(tp, 1)
            pe.wait_ge(hi_ok, TOK)
            pe.wait_ge(lo_ok, TOK)
            pe.wait_ge(blk_ok, 1)
            for c in range(TOK):
                for a, xs in enumerate((xT_hi, xT_lo)):
                    for k in range(KT):
                        last = nc.tensor.matmul(ps_y[:, c * 32:c * 32 + 32], xs[:, k, c * P:(c + 1) * P], gw2[:, k, :],
                                                start=(c == 0 and a == 0 and k == 0), stop=(a == 1 and k == 1),
                                                skip_group_check=True)
            last.then_inc(logit_ok, 1)
            for bt in range(B):
                for i in range(WIN):
                    for jh in range(2):
                        n = (bt * WIN + i) * 2 + jh
                        if n >= 2:
                            pe.wait_ge(qkv_ok, n - 1)
                        for s, (xs, ws) in enumerate(((xW_hi, blk_hi), (xW_lo, blk_hi), (xW_hi, blk_lo))):
                            last = nc.tensor.matmul(misc[n % 2][:, 0:3 * C * WIN], xs[:, jh, (bt * WIN + i) * P:(bt * WIN + i + 1) * P], ws[:, :],
                                                    start=(s == 0), stop=(s == 2))
                        last.then_inc(qkv_ps, 1)

            def gate_up(tile, b, u, par, early):
                if not early:
                    pe.wait_ge(m_ok, u - 1)
                pe.wait_ge(wsplit_lo, tile + 1)
                s = tile % SLOTS
                for a, (ps, done) in enumerate(((guA[par], g_ps), (guB[par], u_ps))):
                    for k in range(KT):
                        w0 = (a * KT + k) * P
                        for q, (ws, xs) in enumerate(((w_hi, xT_hi), (w_hi, xT_lo), (w_lo, xT_hi))):
                            last = nc.tensor.matmul(ps[:, :], ws[:, s, w0:w0 + P], xs[:, k, bass.ds(b * BT, BT)],
                                                    start=(k == 0 and q == 0), stop=(k == KT - 1 and q == 2))
                    last.then_inc(done, 1)

            def down(tile, u, par, first, final, blocks_before):
                pe.wait_ge(ilo_ok, u + 1)
                if first and blocks_before is not None:
                    pe.wait_ge(y_ok, blocks_before)
                s = tile % SLOTS
                for t in range(TILES):
                    for q, (xs, ws) in enumerate(((in_hi, w_hi), (in_hi, w_lo), (in_lo, w_hi))):
                        last = nc.tensor.matmul(ps_y[:, t * H:(t + 1) * H], xs[:, par, t * P:(t + 1) * P],
                                                ws[:, s, UP:WTILE], start=(first and q == 0 and t % 2 == 0),
                                                stop=(final and q == 2), skip_group_check=True)
                return last

            gate_up(0, 0, 0, 0, True)
            gate_up(1, 0, 1, 1, True)
            pe.wait_ge(sig_in, 1)
            for g in range(5):
                m0, n = GROUPS[g]
                U0 = first_unit(g)

                def body(b, last_block, extra):
                    for i in range(n):
                        u = U0 + n * b + i
                        if i + 2 < n:
                            gate_up(m0 + i + 2, b, u + 2, (U0 + i) % 2 if n % 2 == 0 else (u % 2), False)
                        elif not last_block:
                            gate_up(m0 + i + 2 - n, b + 1, u + 2, (U0 + i) % 2 if n % 2 == 0 else (u % 2), False)
                        elif g < 4:
                            gate_up(m0 + i + 2, 0, u + 2, i % 2 if n % 2 == 0 else u % 2, False)
                        before = None if g == 0 and isinstance(b, int) and b == 0 else g * NBLK + b
                        par = i % 2 if n % 2 == 0 else u % 2
                        last = down(m0 + i, u, par, i == 0, i == n - 1, before)
                        last.then_inc(d_ok, 1)
                        if extra:
                            extra(n * b + i)

                def combine_step(s):
                    if s == COMB_AT:
                        pe.wait_ge(route_ok, 1)
                        pe.wait_ge(qkv_ok, 32)
                        for h in range(2):
                            last = nc.tensor.transpose(misc[0][:, h * P:(h + 1) * P], prod[:, 1, h * P:(h + 1) * P], ident[:, :])
                        last.then_inc(combT_ok, 1)

                def tail_step(s):
                    for j in transposes_at(s):
                        bt, i = divmod(j, WIN)
                        pe.wait_ge(attx_ok, 4)
                        if j >= 2:
                            pe.wait_ge(at_sb, j - 1)
                        for h in range(2):
                            a0 = bt * 2048 + i * 256 + h * P
                            last = nc.tensor.transpose(misc[j % 2][:, h * P:(h + 1) * P], xpix[:, a0:a0 + P], ident[:, :])
                        last.then_inc(at_ps, 1)
                    for j in projections_at(s):
                        pe.wait_ge(at_sb, 16)
                        if j >= 2:
                            pe.wait_ge(z_sb, j - 1)
                        first = True
                        for m in range(2 * j, 2 * j + 2):
                            for h in range(2):
                                dst = misc[j % 2][:, ((m % 2) * 2 + h) * P:((m % 2) * 2 + h + 1) * P]
                                nc.tensor.matmul(dst, attT[:, h, m].rearrange("p b r -> p (b r)"), pblk[:, :],
                                                 start=first, stop=False, skip_group_check=True)
                                last = nc.tensor.matmul(dst, ones[0:1, :], prow[0:1, :], start=False, stop=True,
                                                        skip_group_check=True)
                                first = False
                        last.then_inc(z_ps, 1)

                if g in (0, 4):
                    for b in range(NBLK):
                        body(b, b == NBLK - 1, combine_step if g == 0 else tail_step)
                else:
                    with pe.Fori(0, NBLK - 1) as b:
                        body(b, False, None)
                    body(NBLK - 1, True, None)

        @block.vector
        def _(dve):
            mine = Tally()

            def do(ins):
                ins.then_inc(step, 1)
                mine.add()

            def settle():
                dve.wait_ge(step, mine.value())

            def tt(o, a, b, op):
                settle()
                do(nc.vector.tensor_tensor(o, a, b, op))

            for q in range(4):
                dve.wait_ge(x_in[q], 16)
                for j in range(4 * q, 4 * q + 4):
                    do(nc.vector.bn_stats(stats[:, j, :], xw[:, j, :]))
                for j in range(4 * q, 4 * q + 4):
                    settle()
                    do(nc.vector.bn_aggr(mv[:, j, :], stats[:, j, :]))
                settle()
                nc.vector.tensor_scalar_add(mv[:, 4 * q:4 * q + 4, 1], mv[:, 4 * q:4 * q + 4, 1], LN_EPS).then_inc(stat, 1)
            dve.wait_ge(cst_in, 16)
            dve.wait_ge(masks, 3)
            blk = prod[:, 1, 0:3 * C * WIN]
            tt(blk.rearrange("p (c j) -> p c j", j=WIN),
               cst[:, C_QKV:C_QKV + 3 * C].unsqueeze(2).to_broadcast([P, 3 * C, WIN]),
               mask8[:, :].unsqueeze(1).to_broadcast([P, 3 * C, WIN]), ALU.mult)
            settle()
            do(nc.vector.tensor_copy(blk_hi[:, :], blk))
            tt(blk_lo[:, :], blk, blk_hi[:, :].bitcast(F32), ALU.subtract)
            tt(pblk[:, :].rearrange("p (j c) -> p j c", c=C),
               cst[:, C_PROJ:C_PROJ + C].unsqueeze(1).to_broadcast([P, WIN, C]),
               mask8[:, :].unsqueeze(2).to_broadcast([P, WIN, C]), ALU.mult)
            do(nc.vector.tensor_copy(prow[0:1, :].rearrange("p (j c) -> p j c", c=C),
                                     row[0:1, R_PB:R_PB + C].unsqueeze(1).to_broadcast([1, WIN, C])))
            gate = cst[:, C_GATE:C_GATE + KT * NE].rearrange("p (k e) -> p k e", k=KT)
            do(nc.vector.tensor_copy(gw2[:, :, 0:NE], gate))
            settle()
            nc.vector.tensor_tensor(gw2[:, :, NE:2 * NE], gate, gw2[:, :, 0:NE].bitcast(F32), ALU.subtract
                                    ).then_inc(blk_ok, 1)

            def low(j):
                dve.wait_ge(tp, j + 1)
                dve.wait_ge(hi_ok, j + 1)
                for k in range(KT):
                    src = misc[j % 2][:, k * P:(k + 1) * P]
                    nc.vector.tensor_tensor(by_stream(xT_lo, k, j), src.rearrange("p (b c q) -> p b c q", b=B, q=4),
                                            by_stream(xT_hi, k, j).bitcast(F32), ALU.subtract)
                    last = nc.vector.tensor_tensor(by_window(xW_lo, k, j), src.rearrange("p (b w e) -> p b w e", b=B, e=2),
                                                   by_window(xW_hi, k, j).bitcast(F32), ALU.subtract)
                last.then_inc(lo_ok, 1)

            for j in range(TOK):
                dve.wait_ge(rstd_ok, j // 4 + 1)
                nc.vector.tensor_scalar(xw[:, j, :], xw[:, j, :], mv[:, j, 0:1], rstd[:, j:j + 1], ALU.subtract, ALU.mult
                                        ).then_inc(xn_ok, 1)
                if j:
                    low(j - 1)
            low(TOK - 1)

            def area(a, n):
                return prod[:, a // 1024, a % 1024:a % 1024 + n]

            def ce(a):
                return area(a, 256).rearrange("p (c e) -> p c e", e=NE)

            LOG, SC, SFC, SEL, COMB = 0, 256, 512, 768, 1024
            PAIR, GS, GR, SUM = 1280, 1280 + 384, 1280 + 448, 1280 + 512
            dve.wait_ge(logit_ok, 1)
            lg = ps_y[:, 0:512].rearrange("p (c h e) -> p h c e", h=2, e=NE)
            do(nc.vector.tensor_copy(ce(LOG), lg[:, 0]))
            settle()
            nc.vector.tensor_tensor(ce(LOG), lg[:, 1], ce(LOG), ALU.add).then_inc(sig_in, 1)
            dve.wait_ge(sig_ok, 1)
            do(nc.vector.tensor_tensor(ce(SFC), ce(SC), row[:, R_BIAS:R_BIAS + NE].unsqueeze(1).to_broadcast([P, TOK, NE]),
                                       ALU.add))
            v = area(SFC, 256).rearrange("p (n f) -> p n f", f=4)
            pr = area(PAIR, 384).rearrange("p (n s) -> p n s", s=6)
            settle()
            do(nc.vector.tensor_tensor(pr[:, :, 0:2], v[:, :, 0:2], v[:, :, 2:4], ALU.add))
            do(nc.vector.tensor_tensor(pr[:, :, 2:4], v[:, :, 0:4:2], v[:, :, 1:4:2], ALU.add))
            do(nc.vector.tensor_tensor(pr[:, :, 4:5], v[:, :, 0:1], v[:, :, 3:4], ALU.add))
            do(nc.vector.tensor_tensor(pr[:, :, 5:6], v[:, :, 1:2], v[:, :, 2:3], ALU.add))
            settle()
            do(nc.vector.tensor_reduce(area(GS, 64), pr, AX.X, ALU.max))
            settle()

            def ranks(values, n, dst):
                beats = yacc[:, 0:TOK * n * n].rearrange("p (c e f) -> p c e f", c=TOK, e=n)
                for e in range(n):
                    mine_e = values[:, :, e:e + 1]
                    if e:
                        do(nc.vector.tensor_tensor(beats[:, :, e, 0:e], values[:, :, 0:e],
                                                   mine_e.to_broadcast([P, TOK, e]), ALU.is_ge))
                    do(nc.vector.tensor_tensor(beats[:, :, e, e:n], values[:, :, e:n],
                                               mine_e.to_broadcast([P, TOK, n - e]), ALU.is_gt))
                settle()
                do(nc.vector.tensor_reduce(dst, beats, AX.X, ALU.add))
                settle()

            ranks(area(GS, 64).rearrange("p (c g) -> p c g", g=4), 4, area(GR, 64).rearrange("p (c g) -> p c g", g=4))
            do(nc.vector.tensor_scalar(area(GR, 64), area(GR, 64), 2.0, None, ALU.is_lt))
            tt(v, v, area(GR, 64).unsqueeze(2).to_broadcast([P, 64, 4]), ALU.mult)
            settle()
            ranks(ce(SFC), NE, ce(SEL))
            do(nc.vector.tensor_scalar(ce(SEL), ce(SEL), float(TOP), None, ALU.is_lt))
            tt(ce(SEL), ce(SEL), ce(SC), ALU.mult)
            settle()
            do(nc.vector.tensor_reduce(area(SUM, 16), ce(SEL), AX.X, ALU.add))
            settle()
            do(nc.vector.tensor_scalar_add(area(SUM, 16), area(SUM, 16), 1e-20))
            settle()
            do(nc.vector.reciprocal(area(SUM, 16), area(SUM, 16)))
            tt(ce(SEL), ce(SEL), area(SUM, 16).unsqueeze(2).to_broadcast([P, TOK, NE]), ALU.mult)
            settle()
            nc.vector.tensor_scalar(area(COMB, 256).rearrange("p (e c) -> p c e", e=NE), ce(SEL), 2.5, None, ALU.mult
                                    ).then_inc(route_ok, 1)

            def mult(u, par, early, routed):
                dve.wait_ge(u_ps, u + 1)
                if routed:
                    dve.wait_ge(t_ok, u + 1 - first_unit(1))
                else:
                    dve.wait_ge(sil_ok, u + 1)
                if not early:
                    dve.wait_ge(ilo_ok, u - 1)
                nc.vector.tensor_tensor(inter[:, par, :], guB[par][:, :], sil[:, par, :], ALU.mult).then_inc(m_ok, 1)

            def y_sum(b, tiles_done, last=False):
                dve.wait_ge(d_ok, tiles_done)
                acc = yacc[:, bass.ds(b * 1024, 1024)]
                nc.vector.tensor_tensor(acc, ps_y[:, :], acc, ALU.add).then_inc(y_ok, 1)

            for b in range(NBLK):
                for i in range(3):
                    u = 3 * b + i
                    mult(u, u % 2, u < 2, False)
                    if b and i == 1:
                        if b == 1:
                            dve.wait_ge(yacc_in, 32)
                        y_sum(b - 1, 3 * b)

            def parts(b):
                c = b * COMBO
                q = qkv[:, bass.ds(c, 1024)]
                k = qkv[:, bass.ds(c + 1024, 1024)]
                vv = qkv[:, bass.ds(c + 2048, 1024)]
                s = xpix[:, bass.ds(b * 1024, 1024)]
                return q, k, vv, s

            def keys(ap, d=None):
                return ap.rearrange("p (d w k) -> p d k w", d=HD, k=WIN)

            kwq = "p (k w q) -> p k w q"

            def score_ops(b):
                q, k, _, s = parts(b)
                ops = []
                s4 = s.rearrange(kwq, k=WIN, q=WIN)
                for d in range(HD):
                    qd = q.rearrange("p (d t) -> p d t", d=HD)[:, d].rearrange("p (w q) -> p w q", q=WIN)
                    kd = k.rearrange("p (d w k) -> p d k w", d=HD, k=WIN)[:, d]
                    to = s4 if d == 0 else prod[:, d % 2, :].rearrange(kwq, k=WIN, q=WIN)
                    a0 = qd.unsqueeze(1).to_broadcast([P, WIN, 16, WIN])
                    a1 = kd.unsqueeze(3).to_broadcast([P, WIN, 16, WIN])
                    ops.append((lambda to=to, a0=a0, a1=a1: tt(to, a0, a1, ALU.mult)))
                    if d:
                        ops.append((lambda d=d: tt(s, s, prod[:, d % 2, :], ALU.add)))
                return ops

            def soft_ops(b):
                q, _, vv, s = parts(b)
                ops = []
                sk = s.rearrange("p (k t) -> p k t", k=WIN)
                st = s.rearrange("p (k t) -> p t k", k=WIN)
                tm = mx[:, 0, :]

                def top():
                    settle()
                    do(nc.vector.tensor_reduce(tm, st, AX.X, ALU.max))

                def sub():
                    settle()
                    nc.vector.tensor_tensor(sk, sk, tm.unsqueeze(1).to_broadcast([P, WIN, P]), ALU.subtract
                                            ).then_inc(sub_ok, 1)
                ops += [top, sub]
                v3 = vv.rearrange("p (d w t) -> p d w t", d=HD, t=WIN)
                q3 = q.rearrange("p (d w t) -> p d w t", d=HD, t=WIN)
                p3 = prod[:, 0, :].rearrange("p (d w t) -> p d w t", d=HD, t=WIN)
                return ops, v3, q3, p3

            def lepe_ops(b, br):
                _, v3, q3, p3 = soft_ops(b)
                taps = row[:, R_CW:R_CW + 6 * HD].rearrange("p (r t d) -> p r t d", r=2, t=3)[:, br]
                bias = row[:, R_CB:R_CB + 2 * HD].rearrange("p (r d) -> p r d", r=2)[:, br]

                def wide(ap, n):
                    return ap.unsqueeze(2).to_broadcast([P, HD, n])
                q2, v2, p2 = (t.rearrange("p d w t -> p d (w t)") for t in (q3, v3, p3))
                ops = [lambda: tt(q2, v2, wide(taps[:, 1], P), ALU.mult),
                       lambda: tt(q2, q2, wide(bias, P), ALU.add)]
                for t, (o, i) in ((0, (slice(1, 8), slice(0, 7))), (2, (slice(0, 7), slice(1, 8)))):
                    ops.append(lambda t=t: tt(p2, v2, wide(taps[:, t], P), ALU.mult))
                    ops.append(lambda o=o, i=i: tt(q3[:, :, :, o], q3[:, :, :, o], p3[:, :, :, i], ALU.add))
                return ops

            def norm_ops(b):
                _, _, _, s = parts(b)
                sk = s.rearrange("p (k t) -> p k t", k=WIN)
                st = s.rearrange("p (k t) -> p t k", k=WIN)
                rs = mx[:, 1, :]

                def total():
                    dve.wait_ge(exp_ok, b + 1)
                    settle()
                    do(nc.vector.tensor_reduce(rs, st, AX.X, ALU.add))

                def inv():
                    settle()
                    do(nc.vector.reciprocal(rs, rs))
                return [total, inv, lambda: tt(sk, sk, rs.unsqueeze(1).to_broadcast([P, WIN, P]), ALU.mult)]

            def value_ops(b, ks, end):
                q, _, vv, s = parts(b)
                ops = []
                for n, k in enumerate(ks):
                    pk = s.rearrange("p (k t) -> p k t", k=WIN)[:, k].rearrange("p (w q) -> p w q", q=WIN)
                    vk = vv.rearrange("p (d w k) -> p k d w", d=HD, k=WIN)[:, k]
                    to = prod[:, k % 2, :].rearrange("p (d w q) -> p d w q", d=HD, q=WIN)
                    a0 = pk.unsqueeze(1).to_broadcast([P, HD, 16, WIN])
                    a1 = vk.unsqueeze(3).to_broadcast([P, HD, 16, WIN])
                    ops.append((lambda to=to, a0=a0, a1=a1: tt(to, a0, a1, ALU.mult)))
                    if end and n == len(ks) - 1:
                        def fin(k=k):
                            settle()
                            nc.vector.tensor_tensor(q, q, prod[:, k % 2, :], ALU.add).then_inc(att_ok, 1)
                        ops.append(fin)
                    else:
                        ops.append((lambda k=k: tt(q, q, prod[:, k % 2, :], ALU.add)))
                return ops

            dve.wait_ge(qkv_ok, 32)
            dve.wait_ge(xn_out, 16)
            for g in range(1, 4):
                m0, n = GROUPS[g]
                U0 = first_unit(g)

                def unit_block(b, br):
                    if g == 1:
                        ops = score_ops(b)
                        plan = [2, 2, 2, 3, 3, 3]
                    elif g == 2:
                        ops = soft_ops(b)[0] + lepe_ops(b, br) + norm_ops(b) + value_ops(b, range(0, 2), False)
                        plan = [2, 2, 3, 3, 3, 2]
                    else:
                        ops = value_ops(b, range(2, 8), True)
                        plan = [2, 2, 2, 2, 2, 2]
                    assert sum(plan) == len(ops), (sum(plan), len(ops))
                    for i in range(n):
                        u = U0 + n * b + i
                        mult(u, i % 2, False, True)
                        if i == 1:
                            back = NBLK - 1 if isinstance(b, int) and b == 0 else b - 1
                            y_sum(back, U0 + n * b)
                        for _ in range(plan[i]):
                            ops.pop(0)()
                if g == 2:
                    for b in range(NBLK):
                        unit_block(b, b % 2)
                else:
                    unit_block(0, 0)
                    per = 15 if g == 1 else 11
                    with dve.Fori(1, NBLK) as b:
                        mine.enter(b - 1, per)
                        unit_block(b, 0)
                    mine.leave(NBLK - 1)
            m0, n = GROUPS[4]
            U0 = first_unit(4)
            for s in range(n * NBLK):
                b, i = divmod(s, n)
                mult(U0 + s, i % 2, False, True)
                if i == 1:
                    y_sum((b - 1) % NBLK, U0 + n * b)
            Zt = Z.rearrange("p (t c) -> p t c", c=C)
            for hf in range(2):
                if hf == 0:
                    dve.wait_ge(z_sb, 8)
                z = Zt[:, hf * P:(hf + 1) * P, :]
                m = mx[:, hf, :]
                if hf == 0:
                    settle()
                do(nc.vector.tensor_reduce(m, z, AX.X, ALU.add))
                settle()
                do(nc.vector.tensor_scalar(m, m, 1.0 / C, None, ALU.mult))
                settle()
                nc.vector.tensor_tensor(z, z, m.unsqueeze(2).to_broadcast([P, P, C]), ALU.subtract).then_inc(zc_ok, 1)
            for hf in range(2):
                m = mx[:, hf, :]
                dve.wait_ge(sq_ok, hf + 1)
                do(nc.vector.tensor_reduce(m, xpix[:, hf * 2048:(hf + 1) * 2048].rearrange("p (t c) -> p t c", c=C), AX.X, ALU.add))
                settle()
                nc.vector.tensor_scalar(m, m, 1.0 / C, LN_EPS, ALU.mult, ALU.add).then_inc(lnv_ok, 1)
            for hf in range(2):
                z = Zt[:, hf * P:(hf + 1) * P, :]
                dve.wait_ge(lnr_ok, hf + 1)
                tt(z, z, mx[:, hf, :].unsqueeze(2).to_broadcast([P, P, C]), ALU.mult)
                tt(z, z, row[:, R_LNW:R_LNW + C].unsqueeze(1).to_broadcast([P, P, C]), ALU.mult)
                tt(z, z, row[:, R_LNB:R_LNB + C].unsqueeze(1).to_broadcast([P, P, C]), ALU.add)
            dve.wait_ge(xn_in, 16)
            tt(Z, Z, xn2, ALU.add)
            yc = yacc[:, :].rearrange("p (c t) -> p c t", c=C)
            tt(yc, yc, Z.rearrange("p (t c) -> p c t", c=C), ALU.add)
            settle()
            y_sum(NBLK - 1, first_unit(5))


COMB_AT = 5


def transposes_at(s):
    return range(2 * (s - 2), 2 * (s - 1)) if 2 <= s < 10 else range(0)


def projections_at(s):
    return range(4 * (s - 10), 4 * (s - 9)) if 10 <= s < 12 else range(0)


def kernel(**inputs):
    import numpy as np
    import concourse.bacc as bacc
    from concourse.bass_utils import run_bass_kernel_spmd as run

    a = {k: np.asarray(v) for k, v in inputs.items()}
    f = np.float32

    def tiles_up(w):
        w = np.concatenate([w, np.zeros((-len(w) % P, H), w.dtype)])
        return w.reshape(-1, P, KT, P).transpose(0, 3, 2, 1)

    def tiles_down(w):
        w = np.concatenate([w, np.zeros((-len(w) % P, H), w.dtype)])
        return w.reshape(-1, P, H)

    g = np.concatenate([tiles_up(a["L0_ffn_shared_gate_w"]), tiles_up(a["L0_ffn_gate_proj"].reshape(-1, H))])
    u = np.concatenate([tiles_up(a["L0_ffn_shared_up_w"]), tiles_up(a["L0_ffn_up_proj"].reshape(-1, H))])
    d = np.concatenate([tiles_down(a["L0_ffn_shared_down_w"].T),
                        tiles_down(a["L0_ffn_down_proj"].transpose(0, 2, 1).reshape(-1, H))])
    wall = np.ascontiguousarray(np.concatenate([g.reshape(MT, P, KT * P), u.reshape(MT, P, KT * P), d], axis=2))
    taps = np.stack([a["L0_attn_conv_w0"][:, 0, 1, :].T, a["L0_attn_conv_w1"][:, 0, :, 1].T])
    vec = np.concatenate([a["L0_ffn_e_score_correction_bias"], a["L0_attn_ln_w"], a["L0_attn_ln_b"], a["L0_attn_proj_b"],
                          taps.reshape(-1), a["L0_attn_conv_b0"], a["L0_attn_conv_b1"]])
    gate = a["L0_ffn_gate_weight"].T.reshape(KT, P, NE).transpose(1, 0, 2).reshape(P, KT * NE)
    consts = np.ascontiguousarray(np.concatenate(
        [np.tile(a["L0_attn_qkv_w"], (WIN, 1)), np.tile(a["L0_attn_proj_w"], (WIN, 1)), gate,
         np.broadcast_to(vec, (P, len(vec)))], axis=1))

    nc = bacc.Bacc("TRN2", target_bir_lowering=False, num_devices=1)
    arrays = {"x": np.ascontiguousarray(a["L0_attn_x"]), "wall": wall, "consts": consts}
    args = [nc.dram_tensor(k, v.shape, mybir.dt.from_np(v.dtype), kind="ExternalInput").ap() for k, v in arrays.items()]
    o = nc.dram_tensor("out", (B, ROWS, H), F32, kind="ExternalOutput").ap()
    build(nc, *args, o)
    r = run(nc, [arrays], core_ids=[0])
    return r.results[0]["out"]
```

```python
from contextlib import ExitStack

import concourse.bass as bass
from concourse import mybir

F32 = mybir.dt.float32
F32R = mybir.dt.float32r
ALU = mybir.AluOpType
ACT = mybir.ActivationFunctionType
AX = mybir.AxisListType

P = 128
B = 2
ROWS = 1024
H = 256
KT = H // P
T = B * ROWS
C = 16
TOK = H // C
WIN = 8
HD = C // 2
NE = 16
TOP = 6
I = 176
SI = 2 * I
NBLK = 4
BT = T // NBLK
TILES = BT // P
SHARED = -(-SI // P)
ROUTED = NE * I // P
MT = SHARED + ROUTED
UP = 2 * KT * P
WTILE = UP + H
SLOTS = 8
RAW = 3
LN_EPS = 1e-5
GROUPS = [(0, 3), (3, 6), (9, 6), (15, 6), (21, 4)]
COMBO = 3 * HD * P
C_QKV, C_PROJ, C_GATE = 0, 3 * C, 4 * C
C_ROW = C_GATE + KT * NE
R_BIAS, R_LNW, R_LNB, R_PB, R_CW, R_CB = 0, NE, NE + C, NE + 2 * C, NE + 3 * C, NE + 3 * C + 6 * HD
CONSTS = C_ROW + R_CB + 2 * HD


def first_unit(g):
    return sum(n for _, n in GROUPS[:g]) * NBLK


def last_unit(tile):
    g = max(g for g in range(len(GROUPS)) if GROUPS[g][0] <= tile)
    m0, n = GROUPS[g]
    return first_unit(g) + n * (NBLK - 1) + tile - m0


def early_splits(u):
    tile = GROUPS[1][0] + u
    if tile < SLOTS:
        return [tile]
    return [t for t in range(SLOTS, GROUPS[1][0] + GROUPS[1][1]) if last_unit(t - SLOTS) + 1 == u]


class Tally:

    def __init__(self):
        self.n, self.it, self.per = 0, None, 0

    def add(self, k=1):
        self.n += k
        return self.value()

    def value(self):
        return self.n if self.it is None else self.n + self.it * self.per

    def enter(self, it, per):
        self.it, self.per, self.start = it, per, self.n

    def leave(self, times):
        assert self.n - self.start == self.per, (self.n - self.start, self.per)
        self.n += self.per * (times - 1)
        self.it = None


def segments(tile):
    row = (tile - SHARED) * P
    e = row // I
    cut = min(P, (e + 1) * I - row)
    if cut == P:
        return [(0, P // 2, e), (P // 2, P, e)]
    return [(0, cut, e), (cut, P, e + 1)]


def build(nc, x, wall, consts, out):
    ctx = ExitStack()
    with ctx:
        def sb(name, shape, dt=F32):
            return ctx.enter_context(nc.sbuf_tensor(name, shape, dt))

        def sem(name):
            return ctx.enter_context(nc.semaphore(name))

        comb_dram = nc.dram_tensor("comb_dram", [NE, T], F32).ap()
        xn_dram = nc.dram_tensor("xn_dram", [P, TOK * H], F32).ap()

        xpix = sb("xpix", [P, TOK * H])
        yacc = sb("yacc", [P, TOK * H])
        xT_hi = sb("xT_hi", [P, KT, T], F32R)
        xT_lo = sb("xT_lo", [P, KT, T], F32R)
        qkv = sb("qkv", [P, 2 * B * COMBO])
        w_hi = sb("w_hi", [P, SLOTS, WTILE], F32R)
        w_lo = sb("w_lo", [P, SLOTS, WTILE], F32R)
        raw = sb("raw", [P, RAW, WTILE])
        comb = sb("comb", [P, 2, BT])
        sil = sb("sil", [P, 2, BT])
        inter = sb("inter", [P, 2, BT])
        in_hi = sb("in_hi", [P, 2, BT], F32R)
        in_lo = sb("in_lo", [P, 2, BT], F32R)
        prod = sb("prod", [P, 2, HD * P])
        cst = sb("cst", [P, CONSTS])
        ident = sb("ident", [P, P])
        mask8 = sb("mask8", [P, WIN])
        blk_hi = sb("blk_hi", [P, 3 * C * WIN], F32R)
        blk_lo = sb("blk_lo", [P, 3 * C * WIN], F32R)
        pblk = sb("pblk", [P, P])
        prow_hi = sb("prow_hi", [1, P], F32R)
        prow_lo = sb("prow_lo", [1, P], F32R)
        ones = sb("ones", [1, P], F32R)
        gw2 = sb("gw2", [P, KT, 2 * NE], F32R)
        combT = sb("combT", [P, 2, P])
        stats = sb("stats", [P, TOK, 6])
        mv = sb("mv", [P, TOK, 2])
        rstd = sb("rstd", [P, TOK])
        expo = sb("expo", [P, 4])
        mx = sb("mx", [P, 2, P])

        guA = [ctx.enter_context(nc.psum_tensor(f"gate{i}", [P, BT], F32)) for i in range(2)]
        guB = [ctx.enter_context(nc.psum_tensor(f"up{i}", [P, BT], F32)) for i in range(2)]
        ps_y = ctx.enter_context(nc.psum_tensor("ps_y", [P, TILES * H], F32))
        misc = [ctx.enter_context(nc.psum_tensor(f"misc{i}", [P, 512], F32)) for i in range(2)]

        x_in = [sem(f"x_in{i}") for i in range(4)]
        cst_in, yacc_in, xn_out, comb_out = sem("cst_in"), sem("yacc_in"), sem("xn_out"), sem("comb_out")
        xn_in, out_done = sem("xn_in"), sem("out_done")
        raw_in = [sem(f"raw_in{i}") for i in range(RAW)]
        comb_in = [sem(f"comb_in{i}") for i in range(2)]
        masks, gen, stat, rstd_ok, shift_ok, xn_ok = sem("masks"), sem("gen"), sem("stat"), sem("rstd_ok"), sem("shift_ok"), sem("xn_ok")
        proj_ok, gw_ok, blk_ok, tp, hi_ok, lo_ok = sem("proj_ok"), sem("gw_ok"), sem("blk_ok"), sem("tp"), sem("hi_ok"), sem("lo_ok")
        logit_ok, sig_in, sig_ok, route_ok, combT_ok, combT_sb = (
            sem("logit_ok"), sem("sig_in"), sem("sig_ok"), sem("route_ok"), sem("combT_ok"), sem("combT_sb"))
        qkv_ps, qkv_ok = sem("qkv_ps"), sem("qkv_ok")
        wsplit_hi, wsplit_lo = sem("wsplit_hi"), sem("wsplit_lo")
        g_ps, u_ps, sil_ok, t_ok, m_ok, ihi_ok, ilo_ok = (
            sem("g_ps"), sem("u_ps"), sem("sil_ok"), sem("t_ok"), sem("m_ok"), sem("ihi_ok"), sem("ilo_ok"))
        d_ok, y_ps, y_ok = sem("d_ok"), sem("y_ps"), sem("y_ok")
        step, sub_ok, exp_ok, att_ok, attx_ok = sem("step"), sem("sub_ok"), sem("exp_ok"), sem("att_ok"), sem("attx_ok")
        at_ps, at_sb, z_ps, z_sb, sq_ok = sem("at_ps"), sem("at_sb"), sem("z_ps"), sem("z_sb"), sem("sq_ok")
        var_ok, dev_ok, rest_ok = sem("var_ok"), sem("dev_ok"), sem("rest_ok")

        row = cst[:, C_ROW:CONSTS]
        xw = xpix[:, :].rearrange("p (m w) -> p m w", m=TOK)
        attT = qkv[:, 0:4096].rearrange("p (m h r) -> p m h r", h=2, m=16)
        Z = qkv[:, 4096:8192]
        xn2 = qkv[:, 8192:12288]
        x_pix = x.rearrange("b (k m) w -> (b k) (m w)", m=TOK)

        def lanes(ap, j):
            return ap.rearrange("p k (w a b e i) -> p i a k b w e", a=4, b=B, e=2, i=4)[:, j // 4, j % 4]

        def lane_runs():
            return [(64 * l + 16 * a + 8 * b, b, slice(32 * l + a, 32 * l + 32, 4))
                    for l in range(2) for a in range(4) for b in range(B)]

        turn = [misc[0], misc[1], guA[0], guA[1], guB[0], guB[1]]

        block = ctx.enter_context(nc.Block())

        @block.sync
        def _(sp):
            def load_raw(m):
                if m >= RAW:
                    sp.wait_ge(wsplit_hi, m - RAW + 1)
                    sp.wait_ge(wsplit_lo, m - RAW + 1)
                sp.dma_start(raw[:, m % RAW, :], wall[m]).then_inc(raw_in[m % RAW], 16)

            for q in range(4):
                sp.dma_start(xpix[:, q * 1024:(q + 1) * 1024], x_pix[:, q * 1024:(q + 1) * 1024]).then_inc(x_in[q], 16)
                if q == 0:
                    sp.dma_start(cst[:, :], consts).then_inc(cst_in, 16)
            for m in range(RAW):
                load_raw(m)
            sp.wait_ge(xn_ok, TOK)
            sp.dma_start(xn_dram, xpix[:, :]).then_inc(xn_out, 16)
            load_raw(RAW)
            for p0, b, r in lane_runs():
                sp.dma_start(yacc[p0:p0 + WIN, :].rearrange("p (c w) -> p c w", c=C),
                             x[b].rearrange("(c r) w -> r c w", c=C)[r]).then_inc(yacc_in, 16)
            for m in range(RAW + 1, GROUPS[1][0] + GROUPS[1][1]):
                load_raw(m)
            sp.wait_ge(combT_sb, 1)
            sp.dma_start(comb_dram.rearrange("(h e) (c p) -> (e c) h p", h=2, p=P), combT[:, :, :]).then_inc(comb_out, 16)
            sp.wait_ge(comb_out, 16)


            def late_step(s):
                if s == XN_AT:
                    sp.wait_ge(xn_out, 16)
                    sp.wait_ge(attx_ok, 4)
                if XN_AT <= s < XN_AT + 4:
                    for p0, b, r in lane_runs()[4 * (s - XN_AT):4 * (s - XN_AT) + 4]:
                        sp.dma_start(xn2[p0:p0 + WIN, :], xn_dram[64 * b:64 * b + 64, :][r]).then_inc(xn_in, 16)

            for g in range(1, 5):
                m0, n = GROUPS[g]
                r0 = first_unit(g) - first_unit(1)

                def comb_block(b, last, slots_new, extra=None):
                    for i in range(n):
                        if not (slots_new and i < 2):
                            sp.wait_ge(t_ok, r0 + n * b + i - 1)
                        for p0, p1, e in segments(m0 + i):
                            sp.dma_start(comb[p0:p1, i % 2, :],
                                         comb_dram[e:e + 1, bass.ds(b * BT, BT)].to_broadcast([p1 - p0, BT])
                                         ).then_inc(comb_in[i % 2], 16)
                        if last and g < 4 and i < GROUPS[g + 1][1]:
                            load_raw(m0 + n + i)
                        if extra:
                            extra(LATE + n * b + i)
                if g < 4:
                    comb_block(0, False, g == 1)
                    with sp.Fori(1, NBLK - 1) as b:
                        comb_block(b, False, False)
                    comb_block(NBLK - 1, True, False)
                else:
                    for b in range(NBLK):
                        comb_block(b, b == NBLK - 1, False, late_step)
            for p0, s, r in lane_runs():
                sp.wait_ge(rest_ok, NBLK - 1)
                sp.dma_start(out[s].rearrange("(c r) w -> r c w", c=C)[r, 0:TILES * (NBLK - 1), :],
                             yacc[p0:p0 + WIN, 0:(NBLK - 1) * 1024].rearrange("p (c w) -> p c w", w=H)).then_inc(out_done, 16)
            for p0, s, r in lane_runs():
                sp.wait_ge(y_ok, 5 * NBLK)
                sp.dma_start(out[s].rearrange("(c r) w -> r c w", c=C)[r, TILES * (NBLK - 1):C, :],
                             yacc[p0:p0 + WIN, (NBLK - 1) * 1024:NBLK * 1024].rearrange("p (c w) -> p c w", w=H)
                             ).then_inc(out_done, 16)
            sp.wait_ge(out_done, 16 * 16 * 2)

        @block.gpsimd
        def _(pool):
            nc.gpsimd.memset(ident[:, :], 0.0).then_inc(gen, 1)
            nc.gpsimd.memset(mask8[:, :], 1.0).then_inc(gen, 1)
            nc.gpsimd.memset(mx[0:1, 0, :], 1.0).then_inc(masks, 1)
            nc.gpsimd.memset(expo[:, :], -0.5).then_inc(gen, 1)
            pool.wait_ge(gen, 3)
            nc.gpsimd.affine_select(out=ident[:, :], in_=ident[:, :], compare_op=ALU.not_equal, fill=1.0, base=0,
                                    pattern=[[-1, P]], channel_multiplier=1).then_inc(masks, 1)
            nc.gpsimd.affine_select(out=mask8[:, :], in_=mask8[:, :], compare_op=ALU.is_ge, fill=0.0, base=0,
                                    pattern=[[-C, WIN]], channel_multiplier=1).then_inc(gen, 1)
            pool.wait_ge(gen, 4)
            nc.gpsimd.affine_select(out=mask8[:, :], in_=mask8[:, :], compare_op=ALU.is_ge, fill=0.0, base=C - 1,
                                    pattern=[[C, WIN]], channel_multiplier=-1).then_inc(masks, 1)
            for q in range(4):
                pool.wait_ge(stat, q + 1)
                nc.gpsimd.tensor_tensor(rstd[:, 4 * q:4 * q + 4], mv[:, 4 * q:4 * q + 4, 1], expo[:, 0:4], ALU.pow
                                        ).then_inc(rstd_ok, 1)
                pool.wait_ge(rstd_ok, q + 1)
                nc.gpsimd.tensor_tensor(mv[:, 4 * q:4 * q + 4, 0], mv[:, 4 * q:4 * q + 4, 0], rstd[:, 4 * q:4 * q + 4], ALU.mult
                                        ).then_inc(shift_ok, 1)

            def split_lo(m):
                s = m % SLOTS
                pool.wait_ge(wsplit_hi, m + 1)
                nc.gpsimd.tensor_tensor(w_lo[:, s, :], raw[:, m % RAW, :], w_hi[:, s, :].bitcast(F32), ALU.subtract
                                        ).then_inc(wsplit_lo, 1)

            def lo(u, par):
                pool.wait_ge(ihi_ok, u + 1)
                nc.gpsimd.tensor_tensor(in_lo[:, par, :], inter[:, par, :], in_hi[:, par, :].bitcast(F32), ALU.subtract
                                        ).then_inc(ilo_ok, 1)

            for m in range(RAW):
                split_lo(m)
            for u in range(first_unit(1)):
                if u:
                    lo(u - 1, (u - 1) % 2)
                for m in early_splits(u):
                    split_lo(m)
            for g in range(1, 5):
                m0, n = GROUPS[g]
                U0 = first_unit(g)

                def unit_block(b, last):
                    for i in range(n):
                        u = U0 + n * b + i
                        r = u - first_unit(1)
                        pool.wait_ge(sil_ok, u + 1)
                        pool.wait_ge(comb_in[i % 2], (U0 - first_unit(1)) * 16 + n * 16 * b + 32 * (i // 2 + 1))
                        nc.gpsimd.tensor_tensor(sil[:, i % 2, :], sil[:, i % 2, :], comb[:, i % 2, :], ALU.mult
                                                ).then_inc(t_ok, 1)
                        lo(u - 1, (i + 1) % 2)
                        if last and g < 4 and i < GROUPS[g + 1][1]:
                            split_lo(m0 + n + i)
                with pool.Fori(0, NBLK - 1) as b:
                    unit_block(b, False)
                unit_block(NBLK - 1, True)
            lo(first_unit(5) - 1, 1)

        @block.scalar
        def _(act):
            def split_hi(m):
                act.wait_ge(raw_in[m % RAW], 16 * (m // RAW + 1))
                if m >= SLOTS:
                    act.wait_ge(d_ok, last_unit(m - SLOTS) + 1)
                nc.scalar.activation(w_hi[:, m % SLOTS, :], raw[:, m % RAW, :], ACT.Copy).then_inc(wsplit_hi, 1)

            def norm(q):
                act.wait_ge(shift_ok, q + 1)
                for j in range(4 * q, 4 * q + 4):
                    nc.scalar.activation(xw[:, j, :], xw[:, j, :], ACT.Identity, bias=mv[:, j, 0:1], scale=rstd[:, j:j + 1]
                                         ).then_inc(xn_ok, 1)

            def high(j):
                act.wait_ge(tp, j + 1)
                for k in range(KT):
                    src = turn[j % len(turn)][:, k * P:(k + 1) * P].rearrange("p (b w e) -> p b w e", b=B, e=2)
                    last = nc.scalar.activation(lanes(xT_hi, j)[:, k], src, ACT.Copy)
                last.then_inc(hi_ok, 1)

            norm(0)
            norm(1)
            for q in range(4):
                for j in range(4 * q, 4 * q + 4):
                    high(j)
                    if j in WSPLIT_AT:
                        split_hi(WSPLIT_AT.index(j))
                if q < 2:
                    norm(q + 2)
            act.wait_ge(sig_in, 1)
            nc.scalar.activation(prod[:, 0, 256:512], prod[:, 0, 0:256], ACT.Sigmoid).then_inc(sig_ok, 1)

            def qkv_store(n):
                bt, i, jh = n // 16, n // 2 % WIN, n % 2
                act.wait_ge(qkv_ps, n + 1)
                src = misc[n % 2][:, 0:3 * C * WIN].rearrange("p (t r d j) -> p r t d j", t=3, r=2, j=WIN)
                for br in range(2):
                    c0 = (bt * 2 + br) * COMBO
                    dst = qkv[:, c0:c0 + COMBO].rearrange("p (t d k) -> p t d k", t=3, d=HD)
                    if br == 0:
                        dst = dst[:, :, :, i * 16 + jh * 8:i * 16 + jh * 8 + 8]
                    else:
                        dst = dst.rearrange("p t d (j i) -> p i t d j", i=WIN)[:, i, :, :, jh * 8:jh * 8 + 8]
                    last = nc.scalar.activation(dst, src[:, br], ACT.Copy)
                last.then_inc(qkv_ok, 1)

            def silu(u, par, early):
                act.wait_ge(g_ps, u + 1)
                if not early:
                    act.wait_ge(m_ok, u - 1)
                nc.scalar.activation(sil[:, par, :], guA[par][:, :], ACT.Silu).then_inc(sil_ok, 1)

            def hi(u, par, early):
                act.wait_ge(m_ok, u + 1)
                if not early:
                    act.wait_ge(d_ok, u - 1)
                nc.scalar.activation(in_hi[:, par, :], inter[:, par, :], ACT.Copy).then_inc(ihi_ok, 1)

            for u in range(first_unit(1)):
                silu(u, u % 2, u < 2)
                if u:
                    hi(u - 1, (u - 1) % 2, u < 3)
                for n in qkv_jobs(u - 2):
                    qkv_store(n)
                if u == COMB_AT + 2:
                    act.wait_ge(combT_ok, 1)
                    nc.scalar.activation(combT[:, :, :], misc[0][:, 0:2 * P].rearrange("p (h q) -> p h q", h=2),
                                         ACT.Copy).then_inc(combT_sb, 1)
                for m in early_splits(u):
                    split_hi(m)
            for g in range(1, 5):
                m0, n = GROUPS[g]
                U0 = first_unit(g)

                def unit_block(b, last, extra):
                    for i in range(n):
                        u = U0 + n * b + i
                        silu(u, i % 2, False)
                        hi(u - 1, (i + 1) % 2, False)
                        if last and g < 4 and i < GROUPS[g + 1][1]:
                            split_hi(m0 + n + i)
                        if g == 2 and i == 1:
                            act.wait_ge(sub_ok, b + 1)
                            sc = xpix[:, bass.ds(b * 1024, 1024)]
                            nc.scalar.activation(sc, sc, ACT.Exp, scale=HD ** -0.5).then_inc(exp_ok, 1)
                        if extra:
                            extra(n * b + i)
                def late_step(s):
                    if s in ATTX_AT:
                        bt = ATTX_AT.index(s)
                        act.wait_ge(att_ok, 2 * bt + 2)
                        for br in range(2):
                            cb = 2 * bt + br
                            src = qkv[:, cb * COMBO:cb * COMBO + HD * P]
                            dst = xpix[:, bt * 2048:(bt + 1) * 2048].rearrange(
                                "p (i j r d) -> p r d i j", i=WIN, j=16, r=2)[:, br]
                            if br == 0:
                                src = src.rearrange("p (d i j) -> p d i j", d=HD, i=WIN)
                            else:
                                src = src.rearrange("p (d j i) -> p d i j", d=HD, i=WIN)
                            nc.scalar.activation(dst, src, ACT.Copy).then_inc(attx_ok, 1)
                    for j in transposes_at(s - 2):
                        bt, i = divmod(j, WIN)
                        act.wait_ge(at_ps, j + 1)
                        for f in range(2):
                            src = misc[j % 2][:, 0:2 * P].rearrange("p (g n f a) -> p f g n a", g=4, n=WIN, f=2)[:, f]
                            dst = qkv[:, 0:4096].rearrange("p (v a g f e b n) -> p v e b f g n a", v=4, a=4, g=4, f=2, e=2, b=B
                                                           )[:, i % 4, i // 4, bt, f]
                            last_copy = nc.scalar.activation(dst, src, ACT.Copy)
                        last_copy.then_inc(at_sb, 1)
                    for j in projections_at(s - 2):
                        act.wait_ge(z_ps, j + 1)
                        nc.scalar.activation(xpix[:, j * 512:(j + 1) * 512], misc[j % 2][:, :], ACT.Square).then_inc(sq_ok, 1)
                    if s == DEV_AT:
                        act.wait_ge(var_ok, 1)
                        nc.scalar.activation(prod[:, 0, 0:2 * P], mx[:, :, :].rearrange("p h t -> p (h t)"), ACT.Sqrt
                                             ).then_inc(dev_ok, 1)

                if g < 4:
                    with act.Fori(0, NBLK - 1) as b:
                        unit_block(b, False, None)
                    unit_block(NBLK - 1, True, (lambda s: late_step(s - n * (NBLK - 1))) if g == 3 else None)
                else:
                    for b in range(NBLK):
                        unit_block(b, b == NBLK - 1, lambda s: late_step(LATE + s))
            hi(first_unit(5) - 1, 1, False)

        @block.tensor
        def _(pe):
            pe.wait_ge(masks, 3)
            for j in range(TOK):
                pe.wait_ge(xn_ok, j + 1)
                if j >= len(turn):
                    pe.wait_ge(hi_ok, j + 1 - len(turn))
                    pe.wait_ge(lo_ok, j + 1 - len(turn))
                for k in range(KT):
                    last = nc.tensor.transpose(turn[j % len(turn)][:, k * P:(k + 1) * P], xw[:, j, k * P:(k + 1) * P],
                                               ident[:, :])
                last.then_inc(tp, 1)
            pe.wait_ge(hi_ok, TOK)
            pe.wait_ge(lo_ok, TOK)
            pe.wait_ge(gw_ok, 1)
            for c in range(TOK):
                for a, xs in enumerate((xT_hi, xT_lo)):
                    for k in range(KT):
                        last = nc.tensor.matmul(ps_y[:, c * 32:c * 32 + 32], xs[:, k, c * P:(c + 1) * P], gw2[:, k, :],
                                                start=(c == 0 and a == 0 and k == 0), stop=(a == 1 and k == 1),
                                                skip_group_check=True)
            last.then_inc(logit_ok, 1)
            def qkv_job(n):
                bt, i, jh = n // 16, n // 2 % WIN, n % 2
                if n == 0:
                    pe.wait_ge(blk_ok, 1)
                if n >= 2:
                    pe.wait_ge(qkv_ok, n - 1)
                for q, (xs, ws) in enumerate(((xT_hi, blk_hi), (xT_lo, blk_hi), (xT_hi, blk_lo))):
                    last = nc.tensor.matmul(misc[n % 2][:, 0:3 * C * WIN], xs[:, jh, 8 * bt + i:T:16], ws[:, :],
                                            start=(q == 0), stop=(q == 2))
                last.then_inc(qkv_ps, 1)

            def gate_up(tile, b, u, par, early):
                if not early:
                    pe.wait_ge(m_ok, u - 1)
                pe.wait_ge(wsplit_lo, tile + 1)
                s = tile % SLOTS
                for a, (ps, done) in enumerate(((guA[par], g_ps), (guB[par], u_ps))):
                    for k in range(KT):
                        w0 = (a * KT + k) * P
                        for q, (ws, xs) in enumerate(((w_hi, xT_hi), (w_hi, xT_lo), (w_lo, xT_hi))):
                            last = nc.tensor.matmul(ps[:, :], ws[:, s, w0:w0 + P], xs[:, k, bass.ds(b * BT, BT)],
                                                    start=(k == 0 and q == 0), stop=(k == KT - 1 and q == 2))
                    last.then_inc(done, 1)

            def down(tile, u, par, first, final, blocks_before):
                pe.wait_ge(ilo_ok, u + 1)
                if first and blocks_before is not None:
                    pe.wait_ge(y_ok, blocks_before)
                s = tile % SLOTS
                for t in range(TILES):
                    for q, (xs, ws) in enumerate(((in_hi, w_hi), (in_hi, w_lo), (in_lo, w_hi))):
                        last = nc.tensor.matmul(ps_y[:, t * H:(t + 1) * H], xs[:, par, t * P:(t + 1) * P],
                                                ws[:, s, UP:WTILE], start=(first and q == 0 and t % 2 == 0),
                                                stop=(final and q == 2), skip_group_check=True)
                return last

            gate_up(0, 0, 0, 0, True)
            gate_up(1, 0, 1, 1, True)
            pe.wait_ge(sig_in, 1)
            for g in range(5):
                m0, n = GROUPS[g]
                U0 = first_unit(g)

                def body(b, last_block, before_down, behind_down):
                    for i in range(n):
                        u = U0 + n * b + i
                        if i + 2 < n:
                            gate_up(m0 + i + 2, b, u + 2, (U0 + i) % 2 if n % 2 == 0 else (u % 2), False)
                        elif not last_block:
                            gate_up(m0 + i + 2 - n, b + 1, u + 2, (U0 + i) % 2 if n % 2 == 0 else (u % 2), False)
                        elif g < 4:
                            gate_up(m0 + i + 2, 0, u + 2, i % 2 if n % 2 == 0 else u % 2, False)
                        if before_down:
                            before_down(n * b + i)
                        before = None if g == 0 and isinstance(b, int) and b == 0 else g * NBLK + b
                        par = i % 2 if n % 2 == 0 else u % 2
                        last = down(m0 + i, u, par, i == 0, i == n - 1, before)
                        last.then_inc(d_ok, 1)
                        if behind_down:
                            behind_down(n * b + i)

                def first_early(s):
                    for n_job in qkv_jobs(s)[:2]:
                        qkv_job(n_job)

                def first_late(s):
                    for n_job in qkv_jobs(s)[2:]:
                        qkv_job(n_job)
                    if s == COMB_AT:
                        pe.wait_ge(route_ok, 1)
                        pe.wait_ge(qkv_ok, 32)
                        for h in range(2):
                            last = nc.tensor.transpose(misc[0][:, h * P:(h + 1) * P], prod[:, 1, h * P:(h + 1) * P], ident[:, :])
                        last.then_inc(combT_ok, 1)

                def transpose_attention(j):
                    bt, i = divmod(j, WIN)
                    pe.wait_ge(attx_ok, 2 * bt + 2)
                    if j >= 2:
                        pe.wait_ge(at_sb, j - 1)
                    for h in range(2):
                        a0 = bt * 2048 + i * 256 + h * P
                        last = nc.tensor.transpose(misc[j % 2][:, h * P:(h + 1) * P], xpix[:, a0:a0 + P], ident[:, :])
                    last.then_inc(at_ps, 1)

                def project(j):
                    if j == 0:
                        pe.wait_ge(proj_ok, 1)
                        pe.wait_ge(at_sb, 16)
                    if j >= 2:
                        pe.wait_ge(z_sb, j - 1)
                    for q, bias in enumerate((prow_hi, prow_lo)):
                        nc.tensor.matmul(misc[j % 2][:, :], ones[0:1, :], bias[0:1, :].unsqueeze(1).to_broadcast([1, 4, P]),
                                         start=(q == 0), stop=False, skip_group_check=True)
                    for c in range(4):
                        last = nc.tensor.matmul(misc[j % 2][:, c * P:(c + 1) * P], attT[:, 2 * j + c // 2, c % 2], pblk[:, :],
                                                start=False, stop=True, skip_group_check=True)
                    last.then_inc(z_ps, 1)

                def tail_early(s):
                    for j in transposes_at(s)[:2]:
                        transpose_attention(j)
                    for j in projections_at(s)[:1]:
                        project(j)

                def tail_late(s):
                    for j in transposes_at(s)[2:]:
                        transpose_attention(j)
                    for j in projections_at(s)[1:]:
                        project(j)

                if g == 0:
                    for b in range(NBLK):
                        body(b, b == NBLK - 1, first_early, first_late)
                elif g < 4:
                    with pe.Fori(0, NBLK - 1) as b:
                        body(b, False, None, None)
                    if g < 3:
                        body(NBLK - 1, True, None, None)
                    else:
                        body(NBLK - 1, True, lambda s: tail_early(s - n * (NBLK - 1)), lambda s: tail_late(s - n * (NBLK - 1)))
                else:
                    for b in range(NBLK):
                        body(b, b == NBLK - 1, lambda s: tail_early(LATE + s), lambda s: tail_late(LATE + s))

        @block.vector
        def _(dve):
            mine = Tally()

            def do(ins):
                ins.then_inc(step, 1)
                mine.add()

            def settle():
                dve.wait_ge(step, mine.value())

            def tt(o, a, b, op):
                settle()
                do(nc.vector.tensor_tensor(o, a, b, op))

            def norms(q):
                dve.wait_ge(x_in[q], 16)
                for j in range(4 * q, 4 * q + 4):
                    do(nc.vector.bn_stats(stats[:, j, :], xw[:, j, :]))
                for j in range(4 * q, 4 * q + 4):
                    settle()
                    do(nc.vector.bn_aggr(mv[:, j, :], stats[:, j, :]))
                settle()
                do(nc.vector.tensor_scalar(mv[:, 4 * q:4 * q + 4, 0], mv[:, 4 * q:4 * q + 4, 0], -1.0, None, ALU.mult))
                nc.vector.tensor_scalar_add(mv[:, 4 * q:4 * q + 4, 1], mv[:, 4 * q:4 * q + 4, 1], LN_EPS).then_inc(stat, 1)

            def low(j):
                dve.wait_ge(hi_ok, j + 1)
                for k in range(KT):
                    src = turn[j % len(turn)][:, k * P:(k + 1) * P].rearrange("p (b w e) -> p b w e", b=B, e=2)
                    last = nc.vector.tensor_tensor(lanes(xT_lo, j)[:, k], src, lanes(xT_hi, j)[:, k].bitcast(F32), ALU.subtract)
                last.then_inc(lo_ok, 1)

            for q in range(4):
                norms(q)
            dve.wait_ge(cst_in, 16)
            gate = cst[:, C_GATE:C_GATE + KT * NE].rearrange("p (k e) -> p k e", k=KT)
            do(nc.vector.tensor_copy(gw2[:, :, 0:NE], gate))
            settle()
            nc.vector.tensor_tensor(gw2[:, :, NE:2 * NE], gate, gw2[:, :, 0:NE].bitcast(F32), ALU.subtract
                                    ).then_inc(gw_ok, 1)
            for j in range(TOK):
                low(j)
            dve.wait_ge(masks, 3)
            blk = prod[:, 1, 0:3 * C * WIN]
            tt(blk.rearrange("p (c j) -> p c j", j=WIN),
               cst[:, C_QKV:C_QKV + 3 * C].unsqueeze(2).to_broadcast([P, 3 * C, WIN]),
               mask8[:, :].unsqueeze(1).to_broadcast([P, 3 * C, WIN]), ALU.mult)
            settle()
            do(nc.vector.tensor_copy(blk_hi[:, :], blk))
            settle()
            nc.vector.tensor_tensor(blk_lo[:, :], blk, blk_hi[:, :].bitcast(F32), ALU.subtract).then_inc(blk_ok, 1)

            for a, part in enumerate((cst[:, C_PROJ:C_PROJ + C], row[:, R_PB:R_PB + C])):
                mean = stats[:, 0, a:a + 1]
                settle()
                do(nc.vector.tensor_reduce(mean, part, AX.X, ALU.add))
                settle()
                do(nc.vector.tensor_scalar(mean, mean, 1.0 / C, None, ALU.mult))
                settle()
                do(nc.vector.tensor_scalar(part, part, mean, None, ALU.subtract))
            tt(pblk[:, :].rearrange("p (j c) -> p j c", c=C),
               cst[:, C_PROJ:C_PROJ + C].unsqueeze(1).to_broadcast([P, WIN, C]),
               mask8[:, :].unsqueeze(2).to_broadcast([P, WIN, C]), ALU.mult)
            do(nc.vector.tensor_copy(ones[0:1, :], mx[0:1, 0, :]))
            bias_row = row[0:1, R_PB:R_PB + C].unsqueeze(1).to_broadcast([1, WIN, C])
            do(nc.vector.tensor_copy(prow_hi[0:1, :].rearrange("p (j c) -> p j c", c=C), bias_row))
            settle()
            nc.vector.tensor_tensor(prow_lo[0:1, :].rearrange("p (j c) -> p j c", c=C), bias_row,
                                    prow_hi[0:1, :].bitcast(F32).rearrange("p (j c) -> p j c", c=C), ALU.subtract
                                    ).then_inc(proj_ok, 1)

            def area(a, n):
                return prod[:, a // 1024, a % 1024:a % 1024 + n]

            def ce(a):
                return area(a, 256).rearrange("p (c e) -> p c e", e=NE)

            LOG, SC, SFC, SEL, COMB = 0, 256, 512, 768, 1024
            PAIR, GS, GR, SUM = 1280, 1280 + 384, 1280 + 448, 1280 + 512
            dve.wait_ge(logit_ok, 1)
            lg = ps_y[:, 0:512].rearrange("p (c h e) -> p h c e", h=2, e=NE)
            do(nc.vector.tensor_copy(ce(LOG), lg[:, 0]))
            settle()
            nc.vector.tensor_tensor(ce(LOG), lg[:, 1], ce(LOG), ALU.add).then_inc(sig_in, 1)
            routing = []

            def later(make):
                def run_it():
                    settle()
                    do(make())
                routing.append(run_it)

            row_bias = row[:, R_BIAS:R_BIAS + NE].unsqueeze(1).to_broadcast([P, TOK, NE])

            def choice():
                dve.wait_ge(sig_ok, 1)
                do(nc.vector.tensor_tensor(ce(SFC), ce(SC), row_bias, ALU.add))
            routing.append(choice)
            v = area(SFC, 256).rearrange("p (n f) -> p n f", f=4)
            pr = area(PAIR, 384).rearrange("p (n s) -> p n s", s=6)
            for to, left, right in ((slice(0, 2), slice(0, 2), slice(2, 4)), (slice(2, 4), slice(0, 4, 2), slice(1, 4, 2)),
                                    (slice(4, 5), slice(0, 1), slice(3, 4)), (slice(5, 6), slice(1, 2), slice(2, 3))):
                later(lambda to=to, left=left, right=right: nc.vector.tensor_tensor(
                    pr[:, :, to], v[:, :, left], v[:, :, right], ALU.add))
            later(lambda: nc.vector.tensor_reduce(area(GS, 64), pr, AX.X, ALU.max))

            def ranks(values, n, dst):
                beats = xpix[:, 0:TOK * n * n].rearrange("p (c e f) -> p c e f", c=TOK, e=n)

                def compare(e):
                    mine_e = values[:, :, e:e + 1]
                    if e:
                        do(nc.vector.tensor_tensor(beats[:, :, e, 0:e], values[:, :, 0:e],
                                                   mine_e.to_broadcast([P, TOK, e]), ALU.is_ge))
                    else:
                        settle()
                        dve.wait_ge(xn_out, 16)
                    do(nc.vector.tensor_tensor(beats[:, :, e, e:n], values[:, :, e:n],
                                               mine_e.to_broadcast([P, TOK, n - e]), ALU.is_gt))
                for e in range(n):
                    routing.append(lambda e=e: compare(e))
                for c in range(0, TOK, 8):
                    later(lambda c=c: nc.vector.tensor_reduce(dst[:, c:c + 8], beats[:, c:c + 8], AX.X, ALU.add))

            gr = area(GR, 64)
            ranks(area(GS, 64).rearrange("p (c g) -> p c g", g=4), 4, gr.rearrange("p (c g) -> p c g", g=4))
            later(lambda: nc.vector.tensor_scalar(gr, gr, 2.0, None, ALU.is_lt))
            later(lambda: nc.vector.tensor_tensor(v, v, gr.unsqueeze(2).to_broadcast([P, 64, 4]), ALU.mult))
            ranks(ce(SFC), NE, ce(SEL))
            later(lambda: nc.vector.tensor_scalar(ce(SEL), ce(SEL), float(TOP), None, ALU.is_lt))
            later(lambda: nc.vector.tensor_tensor(ce(SEL), ce(SEL), ce(SC), ALU.mult))
            total = area(SUM, 16)
            later(lambda: nc.vector.tensor_reduce(total, ce(SEL), AX.X, ALU.add))
            later(lambda: nc.vector.tensor_scalar_add(total, total, 1e-20))
            later(lambda: nc.vector.reciprocal(total, total))
            later(lambda: nc.vector.tensor_tensor(ce(SEL), ce(SEL), total.unsqueeze(2).to_broadcast([P, TOK, NE]), ALU.mult))

            def weights():
                settle()
                nc.vector.tensor_scalar(area(COMB, 256).rearrange("p (e c) -> p c e", e=NE), ce(SEL), 2.5, None, ALU.mult
                                        ).then_inc(route_ok, 1)
            routing.append(weights)

            def mult(u, par, early, routed):
                dve.wait_ge(u_ps, u + 1)
                if routed:
                    dve.wait_ge(t_ok, u + 1 - first_unit(1))
                else:
                    dve.wait_ge(sil_ok, u + 1)
                if not early:
                    dve.wait_ge(ilo_ok, u - 1)
                nc.vector.tensor_tensor(inter[:, par, :], guB[par][:, :], sil[:, par, :], ALU.mult).then_inc(m_ok, 1)

            def y_sum(b, tiles_done, last=False):
                dve.wait_ge(d_ok, tiles_done)
                acc = yacc[:, bass.ds(b * 1024, 1024)]
                nc.vector.tensor_tensor(acc, ps_y[:, :], acc, ALU.add).then_inc(y_ok, 1)

            for b in range(NBLK):
                for i in range(3):
                    u = 3 * b + i
                    mult(u, u % 2, u < 2, False)
                    if b and i == 1:
                        if b == 1:
                            dve.wait_ge(yacc_in, 16 * 16)
                        y_sum(b - 1, 3 * b)
                    for _ in range(ROUTE_PLAN[u] if u < len(ROUTE_PLAN) else 0):
                        routing.pop(0)()
            assert not routing

            def parts(b):
                c = b * COMBO
                q = qkv[:, bass.ds(c, 1024)]
                k = qkv[:, bass.ds(c + 1024, 1024)]
                vv = qkv[:, bass.ds(c + 2048, 1024)]
                s = xpix[:, bass.ds(b * 1024, 1024)]
                return q, k, vv, s

            def keys(ap, d=None):
                return ap.rearrange("p (d w k) -> p d k w", d=HD, k=WIN)

            kwq = "p (k w q) -> p k w q"

            def score_ops(b):
                q, k, _, s = parts(b)
                ops = []
                s4 = s.rearrange(kwq, k=WIN, q=WIN)
                for d in range(HD):
                    qd = q.rearrange("p (d t) -> p d t", d=HD)[:, d].rearrange("p (w q) -> p w q", q=WIN)
                    kd = k.rearrange("p (d w k) -> p d k w", d=HD, k=WIN)[:, d]
                    to = s4 if d == 0 else prod[:, d % 2, :].rearrange(kwq, k=WIN, q=WIN)
                    a0 = qd.unsqueeze(1).to_broadcast([P, WIN, 16, WIN])
                    a1 = kd.unsqueeze(3).to_broadcast([P, WIN, 16, WIN])
                    ops.append((lambda to=to, a0=a0, a1=a1: tt(to, a0, a1, ALU.mult)))
                    if d:
                        ops.append((lambda d=d: tt(s, s, prod[:, d % 2, :], ALU.add)))
                return ops

            def soft_ops(b):
                q, _, vv, s = parts(b)
                ops = []
                sk = s.rearrange("p (k t) -> p k t", k=WIN)
                st = s.rearrange("p (k t) -> p t k", k=WIN)
                tm = mx[:, 0, :]

                def top():
                    settle()
                    do(nc.vector.tensor_reduce(tm, st, AX.X, ALU.max))

                def sub():
                    settle()
                    nc.vector.tensor_tensor(sk, sk, tm.unsqueeze(1).to_broadcast([P, WIN, P]), ALU.subtract
                                            ).then_inc(sub_ok, 1)
                ops += [top, sub]
                v3 = vv.rearrange("p (d w t) -> p d w t", d=HD, t=WIN)
                q3 = q.rearrange("p (d w t) -> p d w t", d=HD, t=WIN)
                p3 = prod[:, 0, :].rearrange("p (d w t) -> p d w t", d=HD, t=WIN)
                return ops, v3, q3, p3

            def lepe_ops(b, br):
                _, v3, q3, p3 = soft_ops(b)
                taps = row[:, R_CW:R_CW + 6 * HD].rearrange("p (r t d) -> p r t d", r=2, t=3)[:, br]
                bias = row[:, R_CB:R_CB + 2 * HD].rearrange("p (r d) -> p r d", r=2)[:, br]

                def wide(ap, n):
                    return ap.unsqueeze(2).to_broadcast([P, HD, n])
                q2, v2, p2 = (t.rearrange("p d w t -> p d (w t)") for t in (q3, v3, p3))
                ops = [lambda: tt(q2, v2, wide(taps[:, 1], P), ALU.mult),
                       lambda: tt(q2, q2, wide(bias, P), ALU.add)]
                for t, (o, i) in ((0, (slice(1, 8), slice(0, 7))), (2, (slice(0, 7), slice(1, 8)))):
                    ops.append(lambda t=t: tt(p2, v2, wide(taps[:, t], P), ALU.mult))
                    ops.append(lambda o=o, i=i: tt(q3[:, :, :, o], q3[:, :, :, o], p3[:, :, :, i], ALU.add))
                return ops

            def norm_ops(b):
                _, _, _, s = parts(b)
                sk = s.rearrange("p (k t) -> p k t", k=WIN)
                st = s.rearrange("p (k t) -> p t k", k=WIN)
                rs = mx[:, 1, :]

                def total():
                    dve.wait_ge(exp_ok, b + 1)
                    settle()
                    do(nc.vector.tensor_reduce(rs, st, AX.X, ALU.add))

                def inv():
                    settle()
                    do(nc.vector.reciprocal(rs, rs))
                return [total, inv, lambda: tt(sk, sk, rs.unsqueeze(1).to_broadcast([P, WIN, P]), ALU.mult)]

            def value_ops(b, ks, end):
                q, _, vv, s = parts(b)
                ops = []
                for n, k in enumerate(ks):
                    pk = s.rearrange("p (k t) -> p k t", k=WIN)[:, k].rearrange("p (w q) -> p w q", q=WIN)
                    vk = vv.rearrange("p (d w k) -> p k d w", d=HD, k=WIN)[:, k]
                    to = prod[:, k % 2, :].rearrange("p (d w q) -> p d w q", d=HD, q=WIN)
                    a0 = pk.unsqueeze(1).to_broadcast([P, HD, 16, WIN])
                    a1 = vk.unsqueeze(3).to_broadcast([P, HD, 16, WIN])
                    ops.append((lambda to=to, a0=a0, a1=a1: tt(to, a0, a1, ALU.mult)))
                    if end and n == len(ks) - 1:
                        def fin(k=k):
                            settle()
                            nc.vector.tensor_tensor(q, q, prod[:, k % 2, :], ALU.add).then_inc(att_ok, 1)
                        ops.append(fin)
                    else:
                        ops.append((lambda k=k: tt(q, q, prod[:, k % 2, :], ALU.add)))
                return ops

            dve.wait_ge(qkv_ok, 32)
            dve.wait_ge(xn_out, 16)
            for g in range(1, 4):
                m0, n = GROUPS[g]
                U0 = first_unit(g)

                def unit_block(b, br):
                    if g == 1:
                        ops = score_ops(b)
                        plan = [2, 2, 2, 3, 3, 3]
                    elif g == 2:
                        ops = soft_ops(b)[0] + lepe_ops(b, br) + norm_ops(b) + value_ops(b, range(0, 2), False)
                        plan = [2, 2, 3, 3, 3, 2]
                    else:
                        ops = value_ops(b, range(2, 8), True)
                        plan = [2, 2, 2, 2, 2, 2]
                    assert sum(plan) == len(ops), (sum(plan), len(ops))
                    for i in range(n):
                        u = U0 + n * b + i
                        mult(u, i % 2, False, True)
                        if i == 1:
                            back = NBLK - 1 if isinstance(b, int) and b == 0 else b - 1
                            y_sum(back, U0 + n * b)
                        for _ in range(plan[i]):
                            ops.pop(0)()
                if g == 2:
                    for b in range(NBLK):
                        unit_block(b, b % 2)
                else:
                    unit_block(0, 0)
                    per = 15 if g == 1 else 11
                    with dve.Fori(1, NBLK) as b:
                        mine.enter(b - 1, per)
                        unit_block(b, 0)
                    mine.leave(NBLK - 1)
            Zt = Z.rearrange("p (t c) -> p t c", c=C)
            var = mx[:, :, :].rearrange("p h t -> p (h t)")
            dev, newton = prod[:, 0, 0:2 * P], prod[:, 1, 0:2 * P]
            sums = 4 * NBLK - 1

            def late_ops(s):
                ops = []
                if s in (XB_AT, XB_AT + 1):
                    for q in range(2 * (s - XB_AT), 2 * (s - XB_AT) + 2):
                        def add_ln_b(q=q):
                            if q == 0:
                                dve.wait_ge(xn_in, 16 * 16)
                            part = xn2[:, q * 1024:(q + 1) * 1024].rearrange("p (t c) -> p t c", c=C)
                            tt(part, part, row[:, R_LNB:R_LNB + C].unsqueeze(1).to_broadcast([P, 64, C]), ALU.add)
                        ops.append(add_ln_b)
                for j in projections_at(s - 2):
                    def scaled(j=j):
                        dve.wait_ge(sq_ok, j + 1)
                        nc.vector.tensor_tensor(Zt[:, 32 * j:32 * j + 32, :], misc[j % 2][:, :].rearrange("p (t c) -> p t c", c=C),
                                                row[:, R_LNW:R_LNW + C].unsqueeze(1).to_broadcast([P, 32, C]), ALU.mult
                                                ).then_inc(z_sb, 1)

                    def square_sum(j=j):
                        do(nc.vector.tensor_reduce(var[:, 32 * j:32 * j + 32],
                                                   xpix[:, j * 512:(j + 1) * 512].rearrange("p (t c) -> p t c", c=C), AX.X, ALU.add))
                    ops += [scaled, square_sum]
                if s == DEV_AT - 1:
                    def variance():
                        settle()
                        nc.vector.tensor_scalar(var, var, 1.0 / C, LN_EPS, ALU.mult, ALU.add).then_inc(var_ok, 1)
                    ops.append(variance)
                if s in X_SUM_AT:
                    ops += [lambda b=b: add_to_sum(b, xn2) for b in X_SUM_AT[s]]
                if s == DEV_AT + 1:
                    def inverse():
                        dve.wait_ge(dev_ok, 1)
                        do(nc.vector.reciprocal(dev, dev))
                        tt(newton, dev, dev, ALU.mult)
                        tt(newton, newton, var, ALU.mult)
                        settle()
                        do(nc.vector.tensor_scalar(newton, newton, -0.5, 1.5, ALU.mult, ALU.add))
                        tt(dev, dev, newton, ALU.mult)
                    ops.append(inverse)
                if s in (DEV_AT + 1, DEV_AT + 2):
                    for q in range(2 * (s - DEV_AT - 1), 2 * (s - DEV_AT - 1) + 2):
                        def normed(q=q):
                            dve.wait_ge(z_sb, 8)
                            part = Zt[:, 64 * q:64 * q + 64, :]
                            tt(part, part, dev[:, 64 * q:64 * q + 64].unsqueeze(2).to_broadcast([P, 64, C]), ALU.mult)
                        ops.append(normed)
                if s in Z_SUM_AT:
                    ops += [lambda b=b: add_to_sum(b, Z, rest_ok if b < NBLK - 1 else step) for b in Z_SUM_AT[s]]
                return ops

            def add_to_sum(b, tokens, signal=step):
                acc = yacc[:, b * 1024:(b + 1) * 1024].rearrange("p (c t) -> p c t", c=TILES)
                dve.wait_ge(y_ok, sums)
                settle()
                ins = nc.vector.tensor_tensor(acc, acc, tokens.rearrange("p (t c) -> p c t", c=C)[:, TILES * b:TILES * b + TILES, :],
                                              ALU.add)
                if signal is step:
                    do(ins)
                else:
                    ins.then_inc(signal, 1)

            m0, n = GROUPS[4]
            U0 = first_unit(4)
            for s in range(n * NBLK):
                b, i = divmod(s, n)
                mult(U0 + s, i % 2, False, True)
                if i == 1:
                    settle()
                    y_sum((b - 1) % NBLK, U0 + n * b)
                    sums += 1
                for op in late_ops(LATE + s):
                    op()
            settle()
            y_sum(NBLK - 1, first_unit(5))


COMB_AT = 8
ROUTE_PLAN = (7, 9, 5, 4, 4, 5, 5)
WSPLIT_AT = (11, 13, 15)


def qkv_jobs(s):
    return range(4 * s, 4 * s + 4) if 0 <= s < 8 else range(0)


LATE = GROUPS[3][1]
ATTX_AT = (0, 7)
XN_AT = 8
XB_AT = 11
DEV_AT = 17
X_SUM_AT = {13: (0,), 14: (1,), 15: (2,), 16: (3,)}
Z_SUM_AT = {20: (0, 1, 2), 21: (3,)}


def transposes_at(s):
    return {1: range(0, 4), 2: range(4, 8), 8: range(8, 12), 9: range(12, 16)}.get(s, range(0))


def projections_at(s):
    return {11: range(0, 2), 12: range(2, 4), 13: range(4, 6), 14: range(6, 8)}.get(s, range(0))


def kernel(**inputs):
    import numpy as np
    import concourse.bacc as bacc
    from concourse.bass_utils import run_bass_kernel_spmd as run

    a = {k: np.asarray(v) for k, v in inputs.items()}
    f = np.float32

    def tiles_up(w):
        w = np.concatenate([w, np.zeros((-len(w) % P, H), w.dtype)])
        return w.reshape(-1, P, KT, P).transpose(0, 3, 2, 1)

    def tiles_down(w):
        w = np.concatenate([w, np.zeros((-len(w) % P, H), w.dtype)])
        return w.reshape(-1, P, H)

    g = np.concatenate([tiles_up(a["L0_ffn_shared_gate_w"]), tiles_up(a["L0_ffn_gate_proj"].reshape(-1, H))])
    u = np.concatenate([tiles_up(a["L0_ffn_shared_up_w"]), tiles_up(a["L0_ffn_up_proj"].reshape(-1, H))])
    d = np.concatenate([tiles_down(a["L0_ffn_shared_down_w"].T),
                        tiles_down(a["L0_ffn_down_proj"].transpose(0, 2, 1).reshape(-1, H))])
    wall = np.ascontiguousarray(np.concatenate([g.reshape(MT, P, KT * P), u.reshape(MT, P, KT * P), d], axis=2))
    taps = np.stack([a["L0_attn_conv_w0"][:, 0, 1, :].T, a["L0_attn_conv_w1"][:, 0, :, 1].T])
    vec = np.concatenate([a["L0_ffn_e_score_correction_bias"], a["L0_attn_ln_w"], a["L0_attn_ln_b"], a["L0_attn_proj_b"],
                          taps.reshape(-1), a["L0_attn_conv_b0"], a["L0_attn_conv_b1"]])
    gate = a["L0_ffn_gate_weight"].T.reshape(KT, P, NE).transpose(1, 0, 2).reshape(P, KT * NE)
    consts = np.ascontiguousarray(np.concatenate(
        [np.tile(a["L0_attn_qkv_w"], (WIN, 1)), np.tile(a["L0_attn_proj_w"], (WIN, 1)), gate,
         np.broadcast_to(vec, (P, len(vec)))], axis=1))

    nc = bacc.Bacc("TRN2", target_bir_lowering=False, num_devices=1)
    arrays = {"x": np.ascontiguousarray(a["L0_attn_x"]), "wall": wall, "consts": consts}
    args = [nc.dram_tensor(k, v.shape, mybir.dt.from_np(v.dtype), kind="ExternalInput").ap() for k, v in arrays.items()]
    o = nc.dram_tensor("out", (B, ROWS, H), F32, kind="ExternalOutput").ap()
    build(nc, *args, o)
    r = run(nc, [arrays], core_ids=[0])
    return r.results[0]["out"]
```

```python
from contextlib import ExitStack

import concourse.bass as bass
from concourse import mybir

F32 = mybir.dt.float32
F32R = mybir.dt.float32r
ALU = mybir.AluOpType
ACT = mybir.ActivationFunctionType
AX = mybir.AxisListType

P = 128
B = 2
ROWS = 1024
H = 256
KT = H // P
T = B * ROWS
C = 16
TOK = H // C
WIN = 8
HD = C // 2
NE = 16
TOP = 6
I = 176
SI = 2 * I
NBLK = 4
BT = T // NBLK
TILES = BT // P
SHARED = -(-SI // P)
ROUTED = NE * I // P
MT = SHARED + ROUTED
UP = 2 * KT * P
WTILE = UP + H
SLOTS = 8
RAW = 3
LN_EPS = 1e-5
GROUPS = [(0, 3), (3, 6), (9, 6), (15, 6), (21, 4)]
COMBO = 3 * HD * P
C_QKV, C_PROJ, C_GATE = 0, 3 * C, 4 * C
C_ROW = C_GATE + KT * NE
R_BIAS, R_LNW, R_LNB, R_PB, R_CW, R_CB = 0, NE, NE + C, NE + 2 * C, NE + 3 * C, NE + 3 * C + 6 * HD
CONSTS = C_ROW + R_CB + 2 * HD


def first_unit(g):
    return sum(n for _, n in GROUPS[:g]) * NBLK


def last_unit(tile):
    g = max(g for g in range(len(GROUPS)) if GROUPS[g][0] <= tile)
    m0, n = GROUPS[g]
    return first_unit(g) + n * (NBLK - 1) + tile - m0


def early_splits(u):
    early = {3: 3, 4: 4, 5: 5, 7: 6, 8: 7}
    if u in early:
        return [early[u]]
    return [t for t in range(SLOTS, GROUPS[1][0] + GROUPS[1][1]) if last_unit(t - SLOTS) + 2 == u]


class Tally:

    def __init__(self):
        self.n, self.it, self.per = 0, None, 0

    def add(self, k=1):
        self.n += k
        return self.value()

    def value(self):
        return self.n if self.it is None else self.n + self.it * self.per

    def enter(self, it, per):
        self.it, self.per, self.start = it, per, self.n

    def leave(self, times):
        assert self.n - self.start == self.per, (self.n - self.start, self.per)
        self.n += self.per * (times - 1)
        self.it = None


def new_splits(g, block, i):
    at = {NBLK - 2: {2: 0, 5: 1}, NBLK - 1: {2: 2, 3: 3, 4: 4, 5: 5}}.get(block, {})
    return [at[i]] if g < 4 and i in at and at[i] < GROUPS[g + 1][1] else []


def raw_loads(g, block, i):
    at = {NBLK - 2: {0: 0, 1: 1, 2: 2}, NBLK - 1: {0: 3, 1: 4, 3: 5}}.get(block, {})
    return [at[i]] if g < 4 and i in at and at[i] < GROUPS[g + 1][1] else []


def pieces(g, block, i):
    if (g, block, i) == (4, NBLK - 1, GROUPS[4][1] - 1):
        return (slice(0, BT // 2), slice(BT // 2, BT))
    return (slice(0, BT),)


def segments(tile):
    row = (tile - SHARED) * P
    e = row // I
    cut = min(P, (e + 1) * I - row)
    if cut == P:
        return [(0, P // 2, e), (P // 2, P, e)]
    return [(0, cut, e), (cut, P, e + 1)]


def build(nc, x, wall, consts, out):
    ctx = ExitStack()
    with ctx:
        def sb(name, shape, dt=F32):
            return ctx.enter_context(nc.sbuf_tensor(name, shape, dt))

        def sem(name):
            return ctx.enter_context(nc.semaphore(name))

        comb_dram = nc.dram_tensor("comb_dram", [NE, T], F32).ap()
        xn_dram = nc.dram_tensor("xn_dram", [B, ROWS, H], F32).ap()

        xrow = sb("xrow", [P, C * H])
        yacc = sb("yacc", [P, TOK * H])
        xT_hi = sb("xT_hi", [P, KT, T], F32R)
        xT_lo = sb("xT_lo", [P, KT, T], F32R)
        qkv = sb("qkv", [P, 2 * B * COMBO])
        w_hi = sb("w_hi", [P, SLOTS, WTILE], F32R)
        w_lo = sb("w_lo", [P, SLOTS, WTILE], F32R)
        raw = sb("raw", [P, RAW, WTILE])
        comb = sb("comb", [P, 2, BT])
        sil = sb("sil", [P, 2, BT])
        inter = sb("inter", [P, 2, BT])
        in_hi = sb("in_hi", [P, 2, BT], F32R)
        in_lo = sb("in_lo", [P, 2, BT], F32R)
        prod = sb("prod", [P, 2, HD * P])
        cst = sb("cst", [P, CONSTS])
        ident = sb("ident", [P, P])
        mask8 = sb("mask8", [P, WIN])
        blk_hi = sb("blk_hi", [P, 3 * C * WIN], F32R)
        blk_lo = sb("blk_lo", [P, 3 * C * WIN], F32R)
        pblk = sb("pblk", [P, P])
        prow = sb("prow", [2, P], F32R)
        ones = sb("ones", [2, P], F32R)
        combT = sb("combT", [P, 2, P])
        stats = sb("stats", [P, TOK, 6])
        mv = sb("mv", [P, TOK, 2])
        rstd = sb("rstd", [P, TOK])
        expo = sb("expo", [P, 4])
        mx = sb("mx", [P, 2, P])

        guA = [ctx.enter_context(nc.psum_tensor(f"gate{i}", [P, BT], F32)) for i in range(2)]
        guB = [ctx.enter_context(nc.psum_tensor(f"up{i}", [P, BT], F32)) for i in range(2)]
        ps_y = ctx.enter_context(nc.psum_tensor("ps_y", [P, TILES * H], F32))
        misc = [ctx.enter_context(nc.psum_tensor(f"misc{i}", [P, 512], F32)) for i in range(2)]

        x_in = [sem(f"x_in{i}") for i in range(len(XCHUNKS))]
        cst_in, yacc_in, xn_out, comb_out = sem("cst_in"), sem("yacc_in"), sem("xn_out"), sem("comb_out")
        xn_in, out_done, pool_out = sem("xn_in"), sem("out_done"), sem("pool_out")
        raw_in = [sem(f"raw_in{i}") for i in range(RAW)]
        comb_in = [sem(f"comb_in{i}") for i in range(2)]
        masks, zeros, gen, stat = sem("masks"), sem("zeros"), sem("gen"), sem("stat")
        rstd_ok, shift_ok, xn_act, xn_dve = sem("rstd_ok"), sem("shift_ok"), sem("xn_act"), sem("xn_dve")
        proj_ok, gw_ok, blk_ok, tp, hi_ok, lo_ok = sem("proj_ok"), sem("gw_ok"), sem("blk_ok"), sem("tp"), sem("hi_ok"), sem("lo_ok")
        logit_ps, logit_sb, logit_ok, sig_in, sig_ok, route_ok, combT_ok, combT_sb = (
            sem("logit_ps"), sem("logit_sb"), sem("logit_ok"), sem("sig_in"), sem("sig_ok"), sem("route_ok"),
            sem("combT_ok"), sem("combT_sb"))
        qkv_ps, qkv_ok = sem("qkv_ps"), sem("qkv_ok")
        wsplit_hi, wsplit_lo = sem("wsplit_hi"), sem("wsplit_lo")
        last_lo = sem("last_lo")
        g_ps, u_ps, sil_ok, t_ok, m_ok, ihi_ok, ilo_ok = (
            sem("g_ps"), sem("u_ps"), sem("sil_ok"), sem("t_ok"), sem("m_ok"), sem("ihi_ok"), sem("ilo_ok"))
        d_ok, half_ok, y_ok = sem("d_ok"), sem("half_ok"), sem("y_ok")
        step, sub_ok, exp_ok, att_ok, attx_ok = sem("step"), sem("sub_ok"), sem("exp_ok"), sem("att_ok"), sem("attx_ok")
        at_ps, at_sb, z_ps, z_sb, sq_ok = sem("at_ps"), sem("at_sb"), sem("z_ps"), sem("z_sb"), sem("sq_ok")
        var_ok, dev_ok, rest_ok = sem("var_ok"), sem("dev_ok"), sem("rest_ok")

        row = cst[:, C_ROW:CONSTS]
        GW0 = P - 2 * NE
        gw = w_lo[:, SLOTS - 1, 0:KT * (GW0 + P)].rearrange("p (k w) -> p k w", k=KT)
        xw = xrow[:, :].rearrange("p (c w) -> p c w", w=H)
        attT = qkv[:, 0:4096].rearrange("p (m h r) -> p m h r", h=2, m=16)
        Z = qkv[:, 4096:8192]
        xn2 = qkv[:, 8192:12288]

        def lanes(ap, c):
            return ap[:, :, c * P:(c + 1) * P].rearrange("p k (a v b) -> p k b v a", a=4, b=B)

        def rows(ap, b, c0, c1):
            return ap[b].rearrange("(c r) w -> r c w", c=C)[:, c0:c1, :]

        def lane_runs():
            return [(slice(32 * a + b, 32 * a + 32, 2), b, slice(a, 64, 4)) for a in range(4) for b in range(B)]

        def last_block(run, s, r):
            return (out[s].rearrange("(c r) w -> r c w", c=C)[r, TILES * (NBLK - 1):C, :],
                    yacc[run, (NBLK - 1) * 1024:NBLK * 1024].rearrange("p (c w) -> p c w", w=H))

        def bank(c):
            if c < 4:
                return (misc[0], misc[1], ps_y[:, 0:2 * H], ps_y[:, 2 * H:4 * H])[c][:, 0:H]
            return misc[visit_of(c) % 2][:, c % 2 * H:(c % 2 + 1) * H]

        block = ctx.enter_context(nc.Block())

        @block.sync
        def _(sp):
            def load_raw(m):
                if m >= RAW:
                    sp.wait_ge(wsplit_lo, m - RAW + 1)
                sp.dma_start(raw[:, m % RAW, :], wall[m]).then_inc(raw_in[m % RAW], 16)

            for n, (c0, c1) in enumerate(XCHUNKS):
                for b in range(B):
                    sp.dma_start(xw[64 * b:64 * b + 64, c0:c1, :], rows(x, b, c0, c1)).then_inc(x_in[n], 16)
                if n == 1:
                    load_raw(0)
                    sp.dma_start(cst[:, :], consts).then_inc(cst_in, 16)
                if n in (2, 3):
                    load_raw(n - 1)
            load_raw(RAW)
            for run, b, r in lane_runs():
                sp.dma_start(yacc[run, :].rearrange("p (c w) -> p c w", c=C),
                             x[b].rearrange("(c r) w -> r c w", c=C)[r]).then_inc(yacc_in, 16)
            sp.wait_ge(xn_act, C - 2)
            sp.wait_ge(xn_dve, 2)
            for b in range(B):
                sp.dma_start(rows(xn_dram, b, 0, C), xw[64 * b:64 * b + 64, :, :]).then_inc(xn_out, 16)
            for m in range(RAW + 1, GROUPS[1][0] + GROUPS[1][1]):
                load_raw(m)
            sp.wait_ge(combT_sb, 1)
            sp.dma_start(comb_dram.rearrange("(h e) (c p) -> (e c) h p", h=2, p=P), combT[:, :, :]).then_inc(comb_out, 16)
            sp.wait_ge(comb_out, 16)

            def late_step(s):
                if s == XN_AT:
                    sp.wait_ge(xn_out, 32)
                    sp.wait_ge(attx_ok, 4)
                if s in (XN_AT, XN_AT + 1):
                    for run, b, r in lane_runs()[s - XN_AT::2]:
                        sp.dma_start(xn2[run, :], xn_dram[b].rearrange("(k m) w -> k (m w)", m=TOK)[r]).then_inc(xn_in, 16)

            for g in range(1, 5):
                m0, n = GROUPS[g]
                r0 = first_unit(g) - first_unit(1)

                def comb_block(b, blk, slots_new, behind=None):
                    for i in range(n):
                        if not (slots_new and i < 2):
                            sp.wait_ge(t_ok, r0 + n * b + i - 1)
                        for p0, p1, e in segments(m0 + i):
                            sp.dma_start(comb[p0:p1, i % 2, :],
                                         comb_dram[e:e + 1, bass.ds(b * BT, BT)].to_broadcast([p1 - p0, BT])
                                         ).then_inc(comb_in[i % 2], 16)
                        for k in raw_loads(g, blk, i):
                            load_raw(m0 + n + k)
                        if behind:
                            behind(LATE + n * b + i)
                if g < 4:
                    comb_block(0, 0, g == 1)
                    with sp.Fori(1, NBLK - 2) as b:
                        comb_block(b, 1, False)
                    for b in (NBLK - 2, NBLK - 1):
                        comb_block(b, b, False)
                else:
                    for b in range(NBLK):
                        comb_block(b, b, False, late_step)
            for run, s, r in lane_runs():
                sp.wait_ge(rest_ok, NBLK - 1)
                sp.dma_start(out[s].rearrange("(c r) w -> r c w", c=C)[r, 0:TILES * (NBLK - 1), :],
                             yacc[run, 0:(NBLK - 1) * 1024].rearrange("p (c w) -> p c w", w=H)).then_inc(out_done, 16)
            sp.wait_ge(y_ok, 5 * NBLK + 1)
            for run, s, r in lane_runs()[0:3]:
                sp.dma_start(*last_block(run, s, r)).then_inc(out_done, 16)
            sp.wait_ge(out_done, 16 * (8 + 5))
            sp.wait_ge(pool_out, 16 * 3)

        @block.gpsimd
        def _(pool):
            nc.gpsimd.memset(ident[:, :], 0.0).then_inc(gen, 1)
            nc.gpsimd.memset(inter[:, :, 0:GW0 + P], 0.0).then_inc(zeros, 1)
            nc.gpsimd.memset(mask8[:, :], 1.0).then_inc(gen, 1)
            nc.gpsimd.memset(mx[0:2, 0, :], 1.0).then_inc(masks, 1)
            nc.gpsimd.memset(expo[:, :], -0.5).then_inc(gen, 1)
            pool.wait_ge(gen, 3)
            nc.gpsimd.affine_select(out=ident[:, :], in_=ident[:, :], compare_op=ALU.not_equal, fill=1.0, base=0,
                                    pattern=[[-1, P]], channel_multiplier=1).then_inc(masks, 1)
            nc.gpsimd.affine_select(out=mask8[:, :], in_=mask8[:, :], compare_op=ALU.is_ge, fill=0.0, base=0,
                                    pattern=[[-C, WIN]], channel_multiplier=1).then_inc(gen, 1)
            pool.wait_ge(gen, 4)
            nc.gpsimd.affine_select(out=mask8[:, :], in_=mask8[:, :], compare_op=ALU.is_ge, fill=0.0, base=C - 1,
                                    pattern=[[C, WIN]], channel_multiplier=-1).then_inc(masks, 1)

            def power(q):
                pool.wait_ge(stat, q + 1)
                nc.gpsimd.tensor_tensor(rstd[:, 4 * q:4 * q + 4], mv[:, 4 * q:4 * q + 4, 1], expo[:, 0:4], ALU.pow
                                        ).then_inc(rstd_ok, 1)
                pool.wait_ge(rstd_ok, q + 1)
                nc.gpsimd.tensor_tensor(mv[:, 4 * q:4 * q + 4, 0], mv[:, 4 * q:4 * q + 4, 0], rstd[:, 4 * q:4 * q + 4], ALU.mult
                                        ).then_inc(shift_ok, 1)

            def split_lo(m):
                s = m % SLOTS
                pool.wait_ge(wsplit_hi, m + 1)
                nc.gpsimd.tensor_tensor(w_lo[:, s, :], raw[:, m % RAW, :], w_hi[:, s, :].bitcast(F32), ALU.subtract
                                        ).then_inc(wsplit_lo, 1)

            def lo(u, par):
                pool.wait_ge(ihi_ok, u + 1)
                nc.gpsimd.tensor_tensor(in_lo[:, par, :], inter[:, par, :], in_hi[:, par, :].bitcast(F32), ALU.subtract
                                        ).then_inc(ilo_ok, 1)

            power(0)
            split_lo(0)
            split_lo(1)
            power(1)
            split_lo(2)
            power(2)
            for u in range(first_unit(1)):
                if u:
                    lo(u - 1, (u - 1) % 2)
                if u == 1:
                    power(3)
                for m in early_splits(u):
                    split_lo(m)
            for g in range(1, 5):
                m0, n = GROUPS[g]
                U0 = first_unit(g)

                def unit_block(b, blk):
                    for i in range(n):
                        u = U0 + n * b + i
                        pool.wait_ge(comb_in[i % 2], (U0 - first_unit(1)) * 16 + n * 16 * b + 32 * (i // 2 + 1))
                        for w, cols in enumerate(pieces(g, blk, i)):
                            pool.wait_ge(sil_ok, u + 1 + w)
                            nc.gpsimd.tensor_tensor(sil[:, i % 2, cols], sil[:, i % 2, cols], comb[:, i % 2, cols], ALU.mult
                                                    ).then_inc(t_ok, 1)
                            if w == 0 and len(pieces(g, blk, i)) == 1:
                                lo(u - 1, (i + 1) % 2)
                        for k in new_splits(g, blk, i):
                            split_lo(m0 + n + k)
                with pool.Fori(0, NBLK - 2) as b:
                    unit_block(b, 0)
                for b in (NBLK - 2, NBLK - 1):
                    unit_block(b, b)
            pool.wait_ge(ihi_ok, first_unit(5))
            nc.gpsimd.tensor_tensor(in_lo[:, 1, 0:BT // 2], inter[:, 1, 0:BT // 2], in_hi[:, 1, 0:BT // 2].bitcast(F32),
                                    ALU.subtract).then_inc(ilo_ok, 1)
            pool.wait_ge(y_ok, 5 * NBLK + 1)
            for run, s, r in lane_runs()[5:8]:
                nc.gpsimd.dma_start(*last_block(run, s, r)).then_inc(pool_out, 16)

        @block.scalar
        def _(act):
            def split_hi(m):
                act.wait_ge(raw_in[m % RAW], 16 * (m // RAW + 1))
                if m >= SLOTS:
                    act.wait_ge(d_ok, last_unit(m - SLOTS) + 1)
                nc.scalar.activation(w_hi[:, m % SLOTS, :], raw[:, m % RAW, :], ACT.Copy).then_inc(wsplit_hi, 1)

            def norm(q):
                act.wait_ge(shift_ok, q + 1)
                for c in range(4 * q, 4 * q + (2 if q == 0 else 4)):
                    nc.scalar.activation(xw[:, c, :], xw[:, c, :], ACT.Identity, bias=mv[:, c, 0:1], scale=rstd[:, c:c + 1]
                                         ).then_inc(xn_act, 1)

            def high(n):
                act.wait_ge(tp, n + 1)
                for c in VISITS[n]:
                    for k in range(KT):
                        src = bank(c)[:, k * P:(k + 1) * P].rearrange("p (b v a) -> p b v a", b=B, a=4)
                        last = nc.scalar.activation(lanes(xT_hi, c)[:, k], src, ACT.Copy)
                last.then_inc(hi_ok, 1)

            split_hi(0)
            norm(0)
            for n in range(4):
                high(n)
            split_hi(1)
            split_hi(2)

            def qkv_store(n):
                bt, i, jh = n // 16, n // 2 % WIN, n % 2
                act.wait_ge(qkv_ps, n + 1)
                src = misc[n % 2][:, 0:3 * C * WIN].rearrange("p (t r d j) -> p r t d j", t=3, r=2, j=WIN)
                for br in range(2):
                    c0 = (bt * 2 + br) * COMBO
                    dst = qkv[:, c0:c0 + COMBO].rearrange("p (t d k) -> p t d k", t=3, d=HD)
                    if br == 0:
                        dst = dst[:, :, :, i * 16 + jh * 8:i * 16 + jh * 8 + 8]
                    else:
                        dst = dst.rearrange("p t d (j i) -> p i t d j", i=WIN)[:, i, :, :, jh * 8:jh * 8 + 8]
                    last = nc.scalar.activation(dst, src[:, br], ACT.Copy)
                last.then_inc(qkv_ok, 1)

            def silu(u, par, early, parts=(slice(0, BT),)):
                act.wait_ge(g_ps, u + 1)
                if not early:
                    act.wait_ge(m_ok, u - 1)
                for cols in parts:
                    nc.scalar.activation(sil[:, par, cols], guA[par][:, cols], ACT.Silu).then_inc(sil_ok, 1)

            def hi(u, par, early, parts=(slice(0, BT),)):
                if not early:
                    act.wait_ge(d_ok, u - 1)
                for w, cols in enumerate(parts):
                    act.wait_ge(m_ok, u + 1 + w)
                    nc.scalar.activation(in_hi[:, par, cols], inter[:, par, cols], ACT.Copy).then_inc(ihi_ok, 1)

            for u in range(first_unit(1)):
                silu(u, u % 2, u < 2)
                for n in qkv_jobs(u - 2, 0):
                    qkv_store(n)
                if u:
                    hi(u - 1, (u - 1) % 2, u < 3)
                for n in visits_at(u - 2):
                    high(n)
                if u < 3:
                    norm(u + 1)
                if u == LOGITS_AT + 3:
                    act.wait_ge(sig_in, 1)
                    nc.scalar.activation(prod[:, 0, 256:512], prod[:, 0, 0:256], ACT.Sigmoid).then_inc(sig_ok, 1)
                for n in qkv_jobs(u - 2, 1):
                    qkv_store(n)
                if u == LOGITS_AT + 2:
                    act.wait_ge(logit_ps, 1)
                    nc.scalar.activation(prod[:, 0, 0:BT], misc[0][:, :], ACT.Copy).then_inc(logit_sb, 1)
                for m in early_splits(u):
                    split_hi(m)
                for n in qkv_jobs(u - 2, 2):
                    qkv_store(n)
                if u == COMB_AT + 2:
                    act.wait_ge(combT_ok, 1)
                    nc.scalar.activation(combT[:, :, :], misc[0][:, 0:2 * P].rearrange("p (h q) -> p h q", h=2),
                                         ACT.Copy).then_inc(combT_sb, 1)
                if u == first_unit(1) - 1:
                    for n in qkv_jobs(u - 1, 0):
                        qkv_store(n)
            for g in range(1, 5):
                m0, n = GROUPS[g]
                U0 = first_unit(g)

                def unit_block(b, blk, extra):
                    for i in range(n):
                        u = U0 + n * b + i
                        silu(u, i % 2, False, pieces(g, blk, i))
                        hi(u - 1, (i + 1) % 2, False)
                        for k in new_splits(g, blk, i):
                            split_hi(m0 + n + k)
                        if g == 2 and i == 1:
                            act.wait_ge(sub_ok, b + 1)
                            sc = xrow[:, bass.ds(b * 1024, 1024)]
                            nc.scalar.activation(sc, sc, ACT.Exp, scale=HD ** -0.5).then_inc(exp_ok, 1)
                        if extra:
                            extra(n * b + i)

                def late_step(s):
                    if s in ATTX_AT:
                        bt = ATTX_AT.index(s)
                        act.wait_ge(att_ok, 2 * bt + 2)
                        for br in range(2):
                            cb = 2 * bt + br
                            src = qkv[:, cb * COMBO:cb * COMBO + HD * P]
                            dst = xrow[:, bt * 2048:(bt + 1) * 2048].rearrange(
                                "p (i j r d) -> p r d i j", i=WIN, j=16, r=2)[:, br]
                            if br == 0:
                                src = src.rearrange("p (d i j) -> p d i j", d=HD, i=WIN)
                            else:
                                src = src.rearrange("p (d j i) -> p d i j", d=HD, i=WIN)
                            nc.scalar.activation(dst, src, ACT.Copy).then_inc(attx_ok, 1)
                    for j in transposes_at(s - 2):
                        bt, i = divmod(j, WIN)
                        act.wait_ge(at_ps, j + 1)
                        for l in range(2):
                            src = misc[j % 2][:, 0:2 * P].rearrange("p (h c a l) -> p l h c a", h=2, a=4, l=2)[:, l]
                            dst = qkv[:, 0:4096].rearrange("p (v a h l e c b) -> p v e b l h c a", v=4, a=4, h=2, l=2, e=2, b=B
                                                           )[:, i % 4, i // 4, bt, l]
                            last_copy = nc.scalar.activation(dst, src, ACT.Copy)
                        last_copy.then_inc(at_sb, 1)
                    for j in projections_at(s - 2):
                        act.wait_ge(z_ps, j + 1)
                        nc.scalar.activation(xrow[:, j * 512:(j + 1) * 512], misc[j % 2][:, :], ACT.Square).then_inc(sq_ok, 1)
                    if s == DEV_AT:
                        act.wait_ge(var_ok, 1)
                        nc.scalar.activation(prod[:, 0, 0:2 * P], mx[:, :, :].rearrange("p h t -> p (h t)"), ACT.Sqrt
                                             ).then_inc(dev_ok, 1)

                if g < 4:
                    with act.Fori(0, NBLK - 2) as b:
                        unit_block(b, 0, None)
                    unit_block(NBLK - 2, NBLK - 2, None)
                    unit_block(NBLK - 1, NBLK - 1, (lambda s: late_step(s - n * (NBLK - 1))) if g == 3 else None)
                else:
                    for b in range(NBLK):
                        unit_block(b, b, lambda s: late_step(LATE + s))
            hi(first_unit(5) - 1, 1, False, pieces(4, NBLK - 1, GROUPS[4][1] - 1))
            act.wait_ge(y_ok, 5 * NBLK + 1)
            for run, s, r in lane_runs()[3:5]:
                nc.scalar.dma_start(*last_block(run, s, r)).then_inc(out_done, 16)

        @block.tensor
        def _(pe):
            pe.wait_ge(masks, 3)
            for _ in range(WARM_UP):
                nc.tensor.matmul(guA[0][:, 0:P], ident[:, :], ident[:, :], start=True, stop=True)

            def transposes(n):
                if n >= 4:
                    pe.wait_ge(lo_ok, n - 3 if n < 6 else n - 1)
                for c in VISITS[n]:
                    if c in (2, 3):
                        pe.wait_ge(xn_dve, c - 1)
                    else:
                        pe.wait_ge(xn_act, c + 1 if c < 2 else c - 1)
                    for k in range(KT):
                        last = nc.tensor.transpose(bank(c)[:, k * P:(k + 1) * P], xw[:, c, k * P:(k + 1) * P], ident[:, :])
                last.then_inc(tp, 1)

            def gate_logits():
                pe.wait_ge(lo_ok, len(VISITS))
                pe.wait_ge(gw_ok, 1)
                for b in range(NBLK):
                    for xs in (xT_hi, xT_lo):
                        for k in range(KT):
                            w0 = GW0 - 2 * NE * b
                            last = nc.tensor.matmul(misc[0][:, :], gw[:, k, w0:w0 + P], xs[:, k, b * BT:(b + 1) * BT],
                                                    start=(b == 0 and xs is xT_hi and k == 0),
                                                    stop=(b == NBLK - 1 and xs is xT_lo and k == KT - 1))
                last.then_inc(logit_ps, 1)

            def logits_by_token():
                pe.wait_ge(logit_sb, 1)
                for t in range(TILES):
                    last = nc.tensor.transpose(misc[1][:, t * P:(t + 1) * P], prod[:, 0, t * P:(t + 1) * P], ident[:, :])
                last.then_inc(logit_ok, 1)

            def qkv_job(n):
                bt, i, jh = n // 16, n // 2 % WIN, n % 2
                if n == 0:
                    pe.wait_ge(blk_ok, 1)
                if n == JOBS_BEFORE_COMB:
                    pe.wait_ge(combT_sb, 1)
                if n == 1:
                    pe.wait_ge(sig_in, 1)
                if n >= 2:
                    pe.wait_ge(qkv_ok, n - 1)
                for q, (xs, ws) in enumerate(((xT_hi, blk_hi), (xT_lo, blk_hi), (xT_hi, blk_lo))):
                    last = nc.tensor.matmul(misc[n % 2][:, 0:3 * C * WIN], xs[:, jh, 2 * i + bt:T:16], ws[:, :],
                                            start=(q == 0), stop=(q == 2))
                last.then_inc(qkv_ps, 1)

            def gate_up(tile, b, u, par, early, between=None):
                if not early:
                    pe.wait_ge(m_ok, u - 1)
                if tile < SHARED:
                    pe.wait_ge(lo_ok, visit_of(TILES * (b + 1) - 1) + 1)
                pe.wait_ge(wsplit_lo, tile + 1)
                s = tile % SLOTS
                for a, (ps, done) in enumerate(((guA[par], g_ps), (guB[par], u_ps))):
                    for k in range(KT):
                        w0 = (a * KT + k) * P
                        for q, (ws, xs) in enumerate(((w_hi, xT_hi), (w_hi, xT_lo), (w_lo, xT_hi))):
                            last = nc.tensor.matmul(ps[:, :], ws[:, s, w0:w0 + P], xs[:, k, bass.ds(b * BT, BT)],
                                                    start=(k == 0 and q == 0), stop=(k == KT - 1 and q == 2))
                    last.then_inc(done, 1)
                    if between and a == 0:
                        between(u - 2)

            def down(tile, u, par, first, final, blocks_before, parts=1, before_last=False):
                if first and blocks_before is not None:
                    pe.wait_ge(y_ok, blocks_before)
                s = tile % SLOTS
                for t in range(TILES):
                    if t % (TILES // parts) == 0:
                        if parts == 2:
                            pe.wait_ge((ilo_ok, last_lo)[t // 2], (u, 2)[t // 2])
                        elif before_last:
                            pe.wait_ge(last_lo, 1)
                        else:
                            pe.wait_ge(ilo_ok, u + 1)
                    for q, (xs, ws) in enumerate(((in_hi, w_hi), (in_hi, w_lo), (in_lo, w_hi))):
                        last = nc.tensor.matmul(ps_y[:, t * H:(t + 1) * H], xs[:, par, t * P:(t + 1) * P],
                                                ws[:, s, UP:WTILE], start=(first and q == 0 and t % 2 == 0),
                                                stop=(final and q == 2), skip_group_check=True)
                    if parts > 1 and t == TILES // 2 - 1:
                        last.then_inc(half_ok, 1)
                return last

            for n in range(4):
                transposes(n)
            gate_up(0, 0, 0, 0, True)
            gate_up(1, 0, 1, 1, True)
            for n in visits_at(-1):
                transposes(n)
            for g in range(5):
                m0, n = GROUPS[g]
                U0 = first_unit(g)

                def body(b, last_block, before_down, behind_down):
                    for i in range(n):
                        u = U0 + n * b + i
                        par = i % 2 if n % 2 == 0 else u % 2
                        mid = first_between if g == 0 else None
                        if i + 2 < n:
                            gate_up(m0 + i + 2, b, u + 2, par, False, mid)
                        elif not last_block:
                            gate_up(m0 + i + 2 - n, b + 1, u + 2, par, False, mid)
                        elif g < 4:
                            gate_up(m0 + i + 2, 0, u + 2, par, False, mid)
                        if before_down:
                            before_down(n * b + i)
                        before = None if g == 0 and isinstance(b, int) and b == 0 else g * NBLK + b
                        last = down(m0 + i, u, par, i == 0, i == n - 1, before,
                                    len(pieces(g, NBLK - 1 if last_block else 0, i)), (g, last_block, i) == (4, True, n - 2))
                        last.then_inc(d_ok, 1)
                        if behind_down:
                            behind_down(n * b + i)

                def first_between(s):
                    for n_job in qkv_jobs(s, 0):
                        qkv_job(n_job)

                def first_early(s):
                    for n_visit in visits_at(s):
                        transposes(n_visit)
                    if s == LOGITS_AT:
                        gate_logits()
                    if s == LOGITS_AT + 1:
                        logits_by_token()
                    for n_job in qkv_jobs(s, 1):
                        qkv_job(n_job)

                def first_late(s):
                    for n_job in qkv_jobs(s, 2):
                        qkv_job(n_job)
                    if s == COMB_AT:
                        pe.wait_ge(route_ok, 1)
                        pe.wait_ge(qkv_ok, JOBS_BEFORE_COMB - 1)
                        for h in range(2):
                            last = nc.tensor.transpose(misc[0][:, h * P:(h + 1) * P], prod[:, 1, h * P:(h + 1) * P], ident[:, :])
                        last.then_inc(combT_ok, 1)

                def transpose_attention(j):
                    bt, i = divmod(j, WIN)
                    pe.wait_ge(attx_ok, 2 * bt + 2)
                    if j >= 2:
                        pe.wait_ge(at_sb, j - 1)
                    for h in range(2):
                        a0 = bt * 2048 + i * 256 + h * P
                        last = nc.tensor.transpose(misc[j % 2][:, h * P:(h + 1) * P], xrow[:, a0:a0 + P], ident[:, :])
                    last.then_inc(at_ps, 1)

                def project(j):
                    if j == 0:
                        pe.wait_ge(proj_ok, 1)
                        pe.wait_ge(at_sb, 16)
                    if j >= 2:
                        pe.wait_ge(z_sb, j - 1)
                    nc.tensor.matmul(misc[j % 2][:, :], ones[:, :], prow[:, :].unsqueeze(1).to_broadcast([2, 4, P]),
                                     start=True, stop=False, skip_group_check=True)
                    for c in range(4):
                        last = nc.tensor.matmul(misc[j % 2][:, c * P:(c + 1) * P], attT[:, 2 * j + c // 2, c % 2], pblk[:, :],
                                                start=False, stop=True, skip_group_check=True)
                    last.then_inc(z_ps, 1)

                def tail_early(s):
                    for j in transposes_at(s)[:2]:
                        transpose_attention(j)
                    for j in projections_at(s)[:1]:
                        project(j)

                def tail_late(s):
                    for j in transposes_at(s)[2:]:
                        transpose_attention(j)
                    for j in projections_at(s)[1:]:
                        project(j)

                if g == 0:
                    for b in range(NBLK):
                        body(b, b == NBLK - 1, first_early, first_late)
                elif g < 4:
                    with pe.Fori(0, NBLK - 1) as b:
                        body(b, False, None, None)
                    if g < 3:
                        body(NBLK - 1, True, None, None)
                    else:
                        body(NBLK - 1, True, lambda s: tail_early(s - n * (NBLK - 1)), lambda s: tail_late(s - n * (NBLK - 1)))
                else:
                    for b in range(NBLK):
                        body(b, b == NBLK - 1, lambda s: tail_early(LATE + s), lambda s: tail_late(LATE + s))

        @block.vector
        def _(dve):
            mine = Tally()

            def do(ins):
                ins.then_inc(step, 1)
                mine.add()

            def settle(but=0):
                dve.wait_ge(step, mine.value() - but)

            def tt(o, a, b, op, but=0):
                settle(but)
                do(nc.vector.tensor_tensor(o, a, b, op))

            def paired(mults, adds):
                ops = []
                for n in range(0, len(mults), 2):
                    two = len(mults) > n + 1
                    ops.append(lambda n=n: mults[n](1 if n else 0))
                    if two:
                        ops.append(lambda n=n: mults[n + 1](1))
                    ops.append(lambda n=n, two=two: adds[n](1 if two else 0))
                    if two:
                        ops.append(lambda n=n: adds[n + 1](0))
                return ops

            def norms(q):
                for j in range(4 * q, 4 * q + 4):
                    if j in [c0 for c0, _ in XCHUNKS]:
                        dve.wait_ge(x_in[[c0 for c0, _ in XCHUNKS].index(j)], 32)
                    do(nc.vector.bn_stats(stats[:, j, :], xw[:, j, :]))
                settle()
                for j in range(4 * q, 4 * q + 4):
                    do(nc.vector.bn_aggr(mv[:, j, :], stats[:, j, :]))
                settle()
                do(nc.vector.tensor_scalar(mv[:, 4 * q:4 * q + 4, 0], mv[:, 4 * q:4 * q + 4, 0], -1.0, None, ALU.mult))
                nc.vector.tensor_scalar_add(mv[:, 4 * q:4 * q + 4, 1], mv[:, 4 * q:4 * q + 4, 1], LN_EPS).then_inc(stat, 1)

            def low(n):
                dve.wait_ge(hi_ok, n + 1)
                for c in VISITS[n]:
                    for k in range(KT):
                        src = bank(c)[:, k * P:(k + 1) * P].rearrange("p (b v a) -> p b v a", b=B, a=4)
                        last = nc.vector.tensor_tensor(lanes(xT_lo, c)[:, k], src, lanes(xT_hi, c)[:, k].bitcast(F32),
                                                       ALU.subtract)
                last.then_inc(lo_ok, 1)

            dve.wait_ge(zeros, 1)
            do(nc.vector.tensor_copy(gw, inter[:, :, 0:GW0 + P]))
            norms(0)
            dve.wait_ge(shift_ok, 1)
            for c in (2, 3):
                nc.vector.tensor_scalar(xw[:, c, :], xw[:, c, :], rstd[:, c:c + 1], mv[:, c, 0:1], ALU.mult, ALU.add
                                        ).then_inc(xn_dve, 1)
            for n in range(4):
                low(n)
            norms(1)
            dve.wait_ge(cst_in, 16)
            gate = cst[:, C_GATE:C_GATE + KT * NE].rearrange("p (k e) -> p k e", k=KT)
            do(nc.vector.tensor_copy(gw[:, :, GW0:GW0 + NE], gate))
            settle()
            nc.vector.tensor_tensor(gw[:, :, GW0 + NE:P], gate, gw[:, :, GW0:GW0 + NE].bitcast(F32), ALU.subtract
                                    ).then_inc(gw_ok, 1)
            def qkv_weights():
                dve.wait_ge(masks, 3)
                blk = comb[:, 0, 0:3 * C * WIN]
                tt(blk.rearrange("p (c j) -> p c j", j=WIN),
                   cst[:, C_QKV:C_QKV + 3 * C].unsqueeze(2).to_broadcast([P, 3 * C, WIN]),
                   mask8[:, :].unsqueeze(1).to_broadcast([P, 3 * C, WIN]), ALU.mult)
                settle()
                do(nc.vector.tensor_copy(blk_hi[:, :], blk))
                settle()
                nc.vector.tensor_tensor(blk_lo[:, :], blk, blk_hi[:, :].bitcast(F32), ALU.subtract).then_inc(blk_ok, 1)

            def projection_weights():
                for a, part in enumerate((cst[:, C_PROJ:C_PROJ + C], row[:, R_PB:R_PB + C])):
                    mean = stats[:, 0, a:a + 1]
                    settle()
                    do(nc.vector.tensor_reduce(mean, part, AX.X, ALU.add))
                    settle()
                    do(nc.vector.tensor_scalar(mean, mean, 1.0 / C, None, ALU.mult))
                    settle()
                    do(nc.vector.tensor_scalar(part, part, mean, None, ALU.subtract))
                tt(pblk[:, :].rearrange("p (j c) -> p j c", c=C),
                   cst[:, C_PROJ:C_PROJ + C].unsqueeze(1).to_broadcast([P, WIN, C]),
                   mask8[:, :].unsqueeze(2).to_broadcast([P, WIN, C]), ALU.mult)
                do(nc.vector.tensor_copy(ones[:, :], mx[0:2, 0, :]))
                hi_row, lo_row = (mx[0:2, 1, n * C:(n + 1) * C] for n in range(2))
                do(nc.vector.tensor_copy(prow[:, 0:C], row[0:2, R_PB:R_PB + C]))
                tt(lo_row, row[0:2, R_PB:R_PB + C], prow[:, 0:C].bitcast(F32), ALU.subtract)
                do(nc.vector.tensor_scalar(hi_row, prow[:, 0:C].bitcast(F32), ident[0:2, 0:1], None, ALU.mult))
                settle()
                do(nc.vector.tensor_scalar(lo_row, lo_row, ident[0:2, 1:2], None, ALU.mult))
                settle()
                nc.vector.tensor_tensor(prow[:, :].rearrange("p (j c) -> p j c", c=C), hi_row.unsqueeze(1).to_broadcast([2, WIN, C]),
                                        lo_row.unsqueeze(1).to_broadcast([2, WIN, C]), ALU.add).then_inc(proj_ok, 1)

            def area(a, n):
                return prod[:, a // 1024, a % 1024:a % 1024 + n]

            def ce(a):
                return area(a, 256).rearrange("p (c e) -> p c e", e=NE)

            LOG, SC, SFC, SEL, COMB = 0, 256, 512, 768, 1024
            PAIR, GS, GR, SUM = 1280, 1280 + 384, 1280 + 448, 1280 + 512
            def read_logits():
                dve.wait_ge(logit_ok, 1)
                lg = misc[1][:, :].rearrange("p (t b h e) -> p h b t e", t=TILES, b=NBLK, h=2)
                logits = area(LOG, 256).rearrange("p (b t e) -> p b t e", b=NBLK, t=TILES)
                do(nc.vector.tensor_copy(logits, lg[:, 0]))
                settle()
                nc.vector.tensor_tensor(logits, lg[:, 1], logits, ALU.add).then_inc(sig_in, 1)
            routing = []

            def later(make):
                def run_it():
                    settle()
                    do(make())
                routing.append(run_it)

            row_bias = row[:, R_BIAS:R_BIAS + NE].unsqueeze(1).to_broadcast([P, TOK, NE])

            def choice():
                dve.wait_ge(sig_ok, 1)
                do(nc.vector.tensor_tensor(ce(SFC), ce(SC), row_bias, ALU.add))
            routing.append(choice)
            v = area(SFC, 256).rearrange("p (n f) -> p n f", f=4)
            pr = area(PAIR, 384).rearrange("p (n s) -> p n s", s=6)
            for to, left, right in ((slice(0, 2), slice(0, 2), slice(2, 4)), (slice(2, 4), slice(0, 4, 2), slice(1, 4, 2)),
                                    (slice(4, 5), slice(0, 1), slice(3, 4)), (slice(5, 6), slice(1, 2), slice(2, 3))):
                later(lambda to=to, left=left, right=right: nc.vector.tensor_tensor(
                    pr[:, :, to], v[:, :, left], v[:, :, right], ALU.add))
            later(lambda: nc.vector.tensor_reduce(area(GS, 64), pr, AX.X, ALU.max))

            def ranks(values, n, dst):
                beats = xrow[:, 0:TOK * n * n].rearrange("p (c e f) -> p c e f", c=TOK, e=n)

                def compare(e):
                    mine_e = values[:, :, e:e + 1]
                    if e:
                        do(nc.vector.tensor_tensor(beats[:, :, e, 0:e], values[:, :, 0:e],
                                                   mine_e.to_broadcast([P, TOK, e]), ALU.is_ge))
                    else:
                        settle()
                        dve.wait_ge(xn_out, 32)
                    do(nc.vector.tensor_tensor(beats[:, :, e, e:n], values[:, :, e:n],
                                               mine_e.to_broadcast([P, TOK, n - e]), ALU.is_gt))
                for e in range(n):
                    routing.append(lambda e=e: compare(e))
                for c in range(0, TOK, 8):
                    later(lambda c=c: nc.vector.tensor_reduce(dst[:, c:c + 8], beats[:, c:c + 8], AX.X, ALU.add))

            gr = area(GR, 64)
            ranks(area(GS, 64).rearrange("p (c g) -> p c g", g=4), 4, gr.rearrange("p (c g) -> p c g", g=4))
            later(lambda: nc.vector.tensor_scalar(gr, gr, 2.0, None, ALU.is_lt))
            later(lambda: nc.vector.tensor_tensor(v, v, gr.unsqueeze(2).to_broadcast([P, 64, 4]), ALU.mult))
            ranks(ce(SFC), NE, ce(SEL))
            later(lambda: nc.vector.tensor_scalar(ce(SEL), ce(SEL), float(TOP), None, ALU.is_lt))
            later(lambda: nc.vector.tensor_tensor(ce(SEL), ce(SEL), ce(SC), ALU.mult))
            total = area(SUM, 16)
            later(lambda: nc.vector.tensor_reduce(total, ce(SEL), AX.X, ALU.add))
            later(lambda: nc.vector.tensor_scalar_add(total, total, 1e-20))
            later(lambda: nc.vector.reciprocal(total, total))
            later(lambda: nc.vector.tensor_tensor(ce(SEL), ce(SEL), total.unsqueeze(2).to_broadcast([P, TOK, NE]), ALU.mult))

            def weights():
                settle()
                nc.vector.tensor_scalar(area(COMB, 256).rearrange("p (e c) -> p c e", e=NE), ce(SEL), 2.5, None, ALU.mult
                                        ).then_inc(route_ok, 1)
            routing.append(weights)

            def low_part(u, par, cols, more):
                dve.wait_ge(ihi_ok, u + 1 + more)
                nc.vector.tensor_tensor(in_lo[:, par, cols], inter[:, par, cols], in_hi[:, par, cols].bitcast(F32), ALU.subtract
                                        ).then_inc(last_lo, 1)

            def mult(u, par, early, routed, parts=(slice(0, BT),)):
                dve.wait_ge(u_ps, u + 1)
                if not early:
                    dve.wait_ge(ilo_ok, u - 1)
                if len(parts) > 1:
                    low_part(u - 1, 1 - par, slice(0, BT), 0)
                for w, cols in enumerate(parts):
                    if routed:
                        dve.wait_ge(t_ok, u + 1 + w - first_unit(1))
                    else:
                        dve.wait_ge(sil_ok, u + 1)
                    nc.vector.tensor_tensor(inter[:, par, cols], guB[par][:, cols], sil[:, par, cols], ALU.mult
                                            ).then_inc(m_ok, 1)

            def y_sum(b, tiles_done, last=False):
                dve.wait_ge(d_ok, tiles_done)
                acc = yacc[:, bass.ds(b * 1024, 1024)]
                nc.vector.tensor_tensor(acc, ps_y[:, :], acc, ALU.add).then_inc(y_ok, 1)

            def add_to_sum(b, tokens, sums, signal=step):
                acc = yacc[:, b * 1024:(b + 1) * 1024].rearrange("p (c t) -> p c t", c=TILES)
                dve.wait_ge(y_ok, sums)
                settle()
                ins = nc.vector.tensor_tensor(acc, acc, tokens.rearrange("p (t c) -> p c t", c=C)[:, TILES * b:TILES * b + TILES, :],
                                              ALU.add)
                if signal is step:
                    do(ins)
                else:
                    ins.then_inc(signal, 1)

            def add_ln_b(q):
                if q == 0:
                    dve.wait_ge(xn_in, 16 * 8)
                part = xn2[:, q * 1024:(q + 1) * 1024].rearrange("p (t c) -> p t c", c=C)
                tt(part, part, row[:, R_LNB:R_LNB + C].unsqueeze(1).to_broadcast([P, 64, C]), ALU.add)

            for b in range(NBLK):
                for i in range(3):
                    u = 3 * b + i
                    mult(u, u % 2, u < 2, False)
                    for q in visits_at(u - 2):
                        low(q)
                    if b and i == 1:
                        if b == 1:
                            dve.wait_ge(yacc_in, 16 * 8)
                        y_sum(b - 1, 3 * b)
                    if u < 2:
                        norms(u + 2)
                    if u == 2:
                        qkv_weights()
                    if u == LOGITS_AT + 2:
                        projection_weights()
                    if u == LOGITS_AT + 3:
                        read_logits()
                    for _ in range(ROUTE_PLAN.get(u, 0)):
                        routing.pop(0)()
            assert not routing

            def parts(b):
                c = b * COMBO
                q = qkv[:, bass.ds(c, 1024)]
                k = qkv[:, bass.ds(c + 1024, 1024)]
                vv = qkv[:, bass.ds(c + 2048, 1024)]
                s = xrow[:, bass.ds(b * 1024, 1024)]
                return q, k, vv, s

            def keys(ap, d=None):
                return ap.rearrange("p (d w k) -> p d k w", d=HD, k=WIN)

            kwq = "p (k w q) -> p k w q"

            def score_ops(b):
                q, k, _, s = parts(b)
                first, mults, adds = [], [], []
                s4 = s.rearrange(kwq, k=WIN, q=WIN)
                for d in range(HD):
                    qd = q.rearrange("p (d t) -> p d t", d=HD)[:, d].rearrange("p (w q) -> p w q", q=WIN)
                    kd = k.rearrange("p (d w k) -> p d k w", d=HD, k=WIN)[:, d]
                    to = s4 if d == 0 else prod[:, d % 2, :].rearrange(kwq, k=WIN, q=WIN)
                    a0 = qd.unsqueeze(1).to_broadcast([P, WIN, 16, WIN])
                    a1 = kd.unsqueeze(3).to_broadcast([P, WIN, 16, WIN])
                    if d:
                        mults.append(lambda but, to=to, a0=a0, a1=a1: tt(to, a0, a1, ALU.mult, but))
                        adds.append(lambda but, d=d: tt(s, s, prod[:, d % 2, :], ALU.add, but))
                    else:
                        first.append(lambda to=to, a0=a0, a1=a1: tt(to, a0, a1, ALU.mult))
                return first + paired(mults, adds)

            def soft_ops(b):
                q, _, vv, s = parts(b)
                ops = []
                sk = s.rearrange("p (k t) -> p k t", k=WIN)
                st = s.rearrange("p (k t) -> p t k", k=WIN)
                tm = mx[:, 0, :]

                def top():
                    settle()
                    do(nc.vector.tensor_reduce(tm, st, AX.X, ALU.max))

                def sub():
                    settle()
                    nc.vector.tensor_tensor(sk, sk, tm.unsqueeze(1).to_broadcast([P, WIN, P]), ALU.subtract
                                            ).then_inc(sub_ok, 1)
                ops += [top, sub]
                v3 = vv.rearrange("p (d w t) -> p d w t", d=HD, t=WIN)
                q3 = q.rearrange("p (d w t) -> p d w t", d=HD, t=WIN)
                p3 = prod[:, 0, :].rearrange("p (d w t) -> p d w t", d=HD, t=WIN)
                return ops, v3, q3, p3

            def lepe_ops(b, br):
                _, v3, q3, p3 = soft_ops(b)
                taps = row[:, R_CW:R_CW + 6 * HD].rearrange("p (r t d) -> p r t d", r=2, t=3)[:, br]
                bias = row[:, R_CB:R_CB + 2 * HD].rearrange("p (r d) -> p r d", r=2)[:, br]

                def wide(ap, n):
                    return ap.unsqueeze(2).to_broadcast([P, HD, n])
                q2, v2, p2 = (t.rearrange("p d w t -> p d (w t)") for t in (q3, v3, p3))
                ops = [lambda: tt(q2, v2, wide(taps[:, 1], P), ALU.mult),
                       lambda: tt(q2, q2, wide(bias, P), ALU.add)]
                for t, (o, i) in ((0, (slice(1, 8), slice(0, 7))), (2, (slice(0, 7), slice(1, 8)))):
                    ops.append(lambda t=t: tt(p2, v2, wide(taps[:, t], P), ALU.mult))
                    ops.append(lambda o=o, i=i: tt(q3[:, :, :, o], q3[:, :, :, o], p3[:, :, :, i], ALU.add))
                return ops

            def norm_ops(b):
                _, _, _, s = parts(b)
                sk = s.rearrange("p (k t) -> p k t", k=WIN)
                st = s.rearrange("p (k t) -> p t k", k=WIN)
                rs = mx[:, 1, :]

                def total():
                    dve.wait_ge(exp_ok, b + 1)
                    settle()
                    do(nc.vector.tensor_reduce(rs, st, AX.X, ALU.add))

                def inv():
                    settle()
                    do(nc.vector.reciprocal(rs, rs))
                return [total, inv, lambda: tt(sk, sk, rs.unsqueeze(1).to_broadcast([P, WIN, P]), ALU.mult)]

            def value_ops(b, ks, end):
                q, _, vv, s = parts(b)
                mults, adds = [], []
                for n, k in enumerate(ks):
                    pk = s.rearrange("p (k t) -> p k t", k=WIN)[:, k].rearrange("p (w q) -> p w q", q=WIN)
                    vk = vv.rearrange("p (d w k) -> p k d w", d=HD, k=WIN)[:, k]
                    to = prod[:, k % 2, :].rearrange("p (d w q) -> p d w q", d=HD, q=WIN)
                    a0 = pk.unsqueeze(1).to_broadcast([P, HD, 16, WIN])
                    a1 = vk.unsqueeze(3).to_broadcast([P, HD, 16, WIN])
                    mults.append(lambda but, to=to, a0=a0, a1=a1: tt(to, a0, a1, ALU.mult, but))
                    if end and n == len(ks) - 1:
                        def fin(but, k=k):
                            settle(but)
                            nc.vector.tensor_tensor(q, q, prod[:, k % 2, :], ALU.add).then_inc(att_ok, 1)
                        adds.append(fin)
                    else:
                        adds.append(lambda but, k=k: tt(q, q, prod[:, k % 2, :], ALU.add, but))
                return paired(mults, adds)

            dve.wait_ge(qkv_ok, QKV_JOBS)
            for g in range(1, 4):
                m0, n = GROUPS[g]
                U0 = first_unit(g)

                def unit_block(b, br):
                    if g == 1:
                        ops = score_ops(b)
                        plan = [2, 2, 2, 3, 3, 3]
                    elif g == 2:
                        ops = soft_ops(b)[0] + lepe_ops(b, br) + norm_ops(b) + value_ops(b, range(0, 1), False)
                        plan = [2, 2, 2, 3, 2, 2]
                    else:
                        ops = value_ops(b, range(1, 8), True)
                        plan = [2, 2, 3, 2, 3, 2]
                    assert sum(plan) == len(ops), (sum(plan), len(ops))
                    if g == 3 and not (isinstance(b, int) and b == 0):
                        dve.wait_ge(att_ok, b)
                    for i in range(n):
                        u = U0 + n * b + i
                        mult(u, i % 2, False, True)
                        if i == 1:
                            back = NBLK - 1 if isinstance(b, int) and b == 0 else b - 1
                            y_sum(back, U0 + n * b)
                        for _ in range(plan[i]):
                            ops.pop(0)()
                if g == 2:
                    for b in range(NBLK):
                        unit_block(b, b % 2)
                else:
                    unit_block(0, 0)
                    per = 15 if g == 1 else 13
                    with dve.Fori(1, NBLK) as b:
                        mine.enter(b - 1, per)
                        unit_block(b, 0)
                    mine.leave(NBLK - 1)
            Zt = Z.rearrange("p (t c) -> p t c", c=C)
            var = mx[:, :, :].rearrange("p h t -> p (h t)")
            dev, newton = prod[:, 0, 0:2 * P], prod[:, 1, 0:2 * P]
            sums = 4 * NBLK - 1

            def late_ops(s):
                ops = []
                ops += [lambda q=q: add_ln_b(q) for q in LN_B_AT.get(s, ())]
                for j in projections_at(s - 2):
                    def scaled(j=j):
                        dve.wait_ge(sq_ok, j + 1)
                        nc.vector.tensor_tensor(Zt[:, 32 * j:32 * j + 32, :], misc[j % 2][:, :].rearrange("p (t c) -> p t c", c=C),
                                                row[:, R_LNW:R_LNW + C].unsqueeze(1).to_broadcast([P, 32, C]), ALU.mult
                                                ).then_inc(z_sb, 1)

                    def square_sum(j=j):
                        do(nc.vector.tensor_reduce(var[:, 32 * j:32 * j + 32],
                                                   xrow[:, j * 512:(j + 1) * 512].rearrange("p (t c) -> p t c", c=C), AX.X, ALU.add))
                    ops += [scaled, square_sum]
                if s == DEV_AT - 1:
                    def variance():
                        settle()
                        nc.vector.tensor_scalar(var, var, 1.0 / C, LN_EPS, ALU.mult, ALU.add).then_inc(var_ok, 1)
                    ops.append(variance)
                ops += [lambda b=b: add_to_sum(b, xn2, sums) for b in X_SUM_AT.get(s, ())]
                if s == DEV_AT:
                    def inverse():
                        dve.wait_ge(dev_ok, 1)
                        do(nc.vector.reciprocal(dev, dev))
                        tt(newton, dev, dev, ALU.mult)
                        tt(newton, newton, var, ALU.mult)
                        settle()
                        do(nc.vector.tensor_scalar(newton, newton, -0.5, 1.5, ALU.mult, ALU.add))
                        tt(dev, dev, newton, ALU.mult)
                    ops.append(inverse)
                if s in NORM_AT:
                    for q in NORM_AT[s]:
                        def normed(q=q):
                            dve.wait_ge(z_sb, 8)
                            part = Zt[:, 64 * q:64 * q + 64, :]
                            tt(part, part, dev[:, 64 * q:64 * q + 64].unsqueeze(2).to_broadcast([P, 64, C]), ALU.mult)
                        ops.append(normed)
                if s in Z_SUM_AT:
                    ops += [lambda b=b: add_to_sum(b, Z, sums, rest_ok if b < NBLK - 1 else step) for b in Z_SUM_AT[s]]
                return ops

            m0, n = GROUPS[4]
            U0 = first_unit(4)
            for s in range(n * NBLK):
                b, i = divmod(s, n)
                mult(U0 + s, i % 2, False, True, pieces(4, b, i))
                if i == 1:
                    settle()
                    y_sum((b - 1) % NBLK, U0 + n * b)
                    sums += 1
                for op in late_ops(LATE + s):
                    op()
            settle()
            low_part(first_unit(5) - 1, 1, slice(BT // 2, BT), 1)
            for h, (signal, count) in enumerate(((half_ok, 1), (d_ok, first_unit(5)))):
                dve.wait_ge(signal, count)
                acc = yacc[:, (NBLK - 1) * 1024 + h * 512:(NBLK - 1) * 1024 + (h + 1) * 512]
                nc.vector.tensor_tensor(acc, ps_y[:, h * 512:(h + 1) * 512], acc, ALU.add).then_inc(y_ok, 1)

WARM_UP = 16
VISITS = [(c,) for c in range(4)] + [(c, c + 1) for c in range(4, C, 2)]
LOGITS_AT = 3
COMB_AT = 8
QKV_JOBS = B * WIN * 2
JOBS_BEFORE_COMB = 24
ROUTE_PLAN = {6: 10, 7: 12, 8: 8, 9: 9}
XCHUNKS = ((0, 2), (2, 4), (4, 8), (8, 12), (12, 16))


def visit_of(c):
    return [n for n in range(len(VISITS)) if c in VISITS[n]][0]


def visits_at(s):
    return {-1: (4, 5), 1: (6, 7), 2: (8, 9)}.get(s, ())


def qkv_jobs(s, point):
    points = [(4, 2)] + [(step, p) for step in (5, 6, 7) for p in range(3)] + [(8, 0), (8, 1), (9, 0), (9, 1), (9, 2), (10, 0)]
    n = 2 * points.index((s, point)) if (s, point) in points else QKV_JOBS
    return range(n, min(n + 2, QKV_JOBS))


LATE = GROUPS[3][1]
ATTX_AT = (0, 7)
XN_AT = 8
LN_B_AT = {10: (0,), 11: (1, 2), 12: (3,)}
X_SUM_AT = {12: (0,), 13: (1,), 14: (2,), 15: (3,)}
DEV_AT = 16
NORM_AT = {16: (0,), 17: (1, 2), 18: (3,)}
Z_SUM_AT = {18: (0,), 19: (1, 2), 20: (3,)}


def transposes_at(s):
    return {2: range(0, 4), 3: range(4, 8), 8: range(8, 12), 9: range(12, 16)}.get(s, range(0))


def projections_at(s):
    return {10: range(0, 2), 11: range(2, 4), 12: range(4, 6), 13: range(6, 8)}.get(s, range(0))


def kernel(**inputs):
    import numpy as np
    import concourse.bacc as bacc
    from concourse.bass_utils import run_bass_kernel_spmd as run

    a = {k: np.asarray(v) for k, v in inputs.items()}

    def tiles_up(w):
        w = np.concatenate([w, np.zeros((-len(w) % P, H), w.dtype)])
        return w.reshape(-1, P, KT, P).transpose(0, 3, 2, 1)

    def tiles_down(w):
        w = np.concatenate([w, np.zeros((-len(w) % P, H), w.dtype)])
        return w.reshape(-1, P, H)

    g = np.concatenate([tiles_up(a["L0_ffn_shared_gate_w"]), tiles_up(a["L0_ffn_gate_proj"].reshape(-1, H))])
    u = np.concatenate([tiles_up(a["L0_ffn_shared_up_w"]), tiles_up(a["L0_ffn_up_proj"].reshape(-1, H))])
    d = np.concatenate([tiles_down(a["L0_ffn_shared_down_w"].T),
                        tiles_down(a["L0_ffn_down_proj"].transpose(0, 2, 1).reshape(-1, H))])
    wall = np.ascontiguousarray(np.concatenate([g.reshape(MT, P, KT * P), u.reshape(MT, P, KT * P), d], axis=2))
    taps = np.stack([a["L0_attn_conv_w0"][:, 0, 1, :].T, a["L0_attn_conv_w1"][:, 0, :, 1].T])
    vec = np.concatenate([a["L0_ffn_e_score_correction_bias"], a["L0_attn_ln_w"], a["L0_attn_ln_b"], a["L0_attn_proj_b"],
                          taps.reshape(-1), a["L0_attn_conv_b0"], a["L0_attn_conv_b1"]])
    gate = a["L0_ffn_gate_weight"].T.reshape(KT, P, NE).transpose(1, 0, 2).reshape(P, KT * NE)
    consts = np.ascontiguousarray(np.concatenate(
        [np.tile(a["L0_attn_qkv_w"], (WIN, 1)), np.tile(a["L0_attn_proj_w"], (WIN, 1)), gate,
         np.broadcast_to(vec, (P, len(vec)))], axis=1))

    nc = bacc.Bacc("TRN2", target_bir_lowering=False, num_devices=1)
    arrays = {"x": np.ascontiguousarray(a["L0_attn_x"]), "wall": wall, "consts": consts}
    args = [nc.dram_tensor(k, v.shape, mybir.dt.from_np(v.dtype), kind="ExternalInput").ap() for k, v in arrays.items()]
    o = nc.dram_tensor("out", (B, ROWS, H), F32, kind="ExternalOutput").ap()
    build(nc, *args, o)
    r = run(nc, [arrays], core_ids=[0])
    return r.results[0]["out"]
```
